# Optimizing a Trainium2 kernel written in Bass

```python
import numpy as np
import jax
import jax.numpy as jnp

def _softmax(x, axis=-1):
    return jax.nn.softmax(x, axis=axis)

def _gelu(x):
    return jax.nn.gelu(x, approximate=True)

def _silu(x):
    return jax.nn.silu(x)

def _sigmoid(x):
    return jax.nn.sigmoid(x)

def _layernorm(x, axis=-1, eps=1e-05):
    m = jnp.mean(x, axis=axis, keepdims=True)
    v = jnp.var(x, axis=axis, keepdims=True)
    return (x - m) / jnp.sqrt(v + eps)

def _scatter_add(tgt, idx, src, axis=0):
    return tgt.at[idx].add(src)

def _segment_sum(src, seg, n):
    return jax.ops.segment_sum(src, seg, n)
kernel_name = 'mk_recurrent_d1_jaxref_r8_54c15f'

def setup_inputs(seed: int=0):
    np.random.seed(seed)
    _w = jnp.asarray

    def _L0_attn_setup():
        import jax, jax.numpy as jnp
        import numpy as np
        NF4 = jnp.array([-1.0, -0.6961928009986877, -0.5250730514526367, -0.39491748809814453, -0.28444138169288635, -0.18477343022823334, -0.09105003625154495, 0.0, 0.07958029955625534, 0.16093020141124725, 0.24611230194568634, 0.33791524171829224, 0.44070982933044434, 0.5626170039176941, 0.7229568362236023, 1.0], dtype=jnp.float32)
        BLOCK = 64

        def _dequant(codes, scales):
            w = NF4[codes]
            O, I = w.shape
            w = w.reshape(O, I // BLOCK, BLOCK) * scales[:, :, None]
            return w.reshape(O, I)

        def _lin_lora(x, W, A, B):
            base = jnp.einsum('bsh,oh->bso', x, W)
            lora = jnp.einsum('bsr,or->bso', jnp.einsum('bsh,rh->bsr', x, A), B)
            return base + lora
        H, I, R, BT, S = (512, 1792, 16, 2, 256)
        key = jax.random.key(seed)
        ks = jax.random.split(key, 12)
        x = jax.random.normal(ks[0], (BT, S, H), jnp.float32)
        codes_attn = jax.random.randint(ks[1], (4, H, H), 0, 16, jnp.int32)
        scales_attn = jax.random.uniform(ks[2], (4, H, H // BLOCK), jnp.float32) * 0.02
        codes_gu = jax.random.randint(ks[3], (2, I, H), 0, 16, jnp.int32)
        scales_gu = jax.random.uniform(ks[4], (2, I, H // BLOCK), jnp.float32) * 0.02
        codes_down = jax.random.randint(ks[5], (H, I), 0, 16, jnp.int32)
        scales_down = jax.random.uniform(ks[6], (H, I // BLOCK), jnp.float32) * 0.02
        lora_A_h = jax.random.normal(ks[7], (6, R, H), jnp.float32) * 0.02
        lora_A_down = jax.random.normal(ks[8], (R, I), jnp.float32) * 0.02
        lora_B_attn = jax.random.normal(ks[9], (4, H, R), jnp.float32) * 0.02
        lora_B_gu = jax.random.normal(ks[10], (2, I, R), jnp.float32) * 0.02
        lora_B_down = jax.random.normal(ks[11], (H, R), jnp.float32) * 0.02
        return dict(x=x, codes_attn=codes_attn, scales_attn=scales_attn, codes_gu=codes_gu, scales_gu=scales_gu, codes_down=codes_down, scales_down=scales_down, lora_A_h=lora_A_h, lora_A_down=lora_A_down, lora_B_attn=lora_B_attn, lora_B_gu=lora_B_gu, lora_B_down=lora_B_down)
    _L0_attn_in = _L0_attn_setup()

    def _L0_ffn_setup():
        import jax, jax.numpy as jnp
        import numpy as np
        B, S, D = (4, 256, 512)
        NUM_EXPERTS, TOP_K = (3, 2)

        def _expert_outputs(h, w1, b1, w2, b2):
            pre = jnp.einsum('bsd,edf->ebsf', h, w1) + b1[:, None, None, :]
            act = jnp.stack([jnp.tanh(pre[0]), jax.nn.gelu(pre[1], approximate=False), jax.nn.silu(pre[2])])
            return jnp.einsum('ebsf,efd->ebsd', act, w2) + b2[:, None, None, :]
        key = jax.random.key(seed)
        ks = jax.random.split(key, 8)
        scale_in = 1.0 / np.sqrt(D)
        scale_gate = 1.0 / np.sqrt(D + 1)
        return {'h': jax.random.normal(ks[0], (B, S, D), dtype=jnp.float32), 'gate_w': jax.random.uniform(ks[1], (D + 1, NUM_EXPERTS), minval=-scale_gate, maxval=scale_gate, dtype=jnp.float32), 'gate_b': jnp.zeros((NUM_EXPERTS,), dtype=jnp.float32), 'w1': jax.random.uniform(ks[2], (NUM_EXPERTS, D, D), minval=-scale_in, maxval=scale_in, dtype=jnp.float32), 'b1': jnp.zeros((NUM_EXPERTS, D), dtype=jnp.float32), 'w2': jax.random.uniform(ks[3], (NUM_EXPERTS, D, D), minval=-scale_in, maxval=scale_in, dtype=jnp.float32), 'b2': jnp.zeros((NUM_EXPERTS, D), dtype=jnp.float32)}
    _L0_ffn_in = _L0_ffn_setup()
    _d = {'L0_attn_x': _L0_attn_in['x'], 'L0_attn_codes_attn': _L0_attn_in['codes_attn'], 'L0_attn_scales_attn': _L0_attn_in['scales_attn'], 'L0_attn_codes_gu': _L0_attn_in['codes_gu'], 'L0_attn_scales_gu': _L0_attn_in['scales_gu'], 'L0_attn_codes_down': _L0_attn_in['codes_down'], 'L0_attn_scales_down': _L0_attn_in['scales_down'], 'L0_attn_lora_A_h': _L0_attn_in['lora_A_h'], 'L0_attn_lora_A_down': _L0_attn_in['lora_A_down'], 'L0_attn_lora_B_attn': _L0_attn_in['lora_B_attn'], 'L0_attn_lora_B_gu': _L0_attn_in['lora_B_gu'], 'L0_attn_lora_B_down': _L0_attn_in['lora_B_down'], 'L0_ffn_gate_w': _L0_ffn_in['gate_w'], 'L0_ffn_gate_b': _L0_ffn_in['gate_b'], 'L0_ffn_w1': _L0_ffn_in['w1'], 'L0_ffn_b1': _L0_ffn_in['b1'], 'L0_ffn_w2': _L0_ffn_in['w2'], 'L0_ffn_b2': _L0_ffn_in['b2']}
    _x0 = _d['L0_attn_x']
    _d['L0_attn_x'] = jax.random.normal(jax.random.fold_in(jax.random.key(seed), 1), (2, 1024, 512), dtype=_x0.dtype)
    del _x0
    return _d

def reference(L0_attn_x, L0_attn_codes_attn, L0_attn_scales_attn, L0_attn_codes_gu, L0_attn_scales_gu, L0_attn_codes_down, L0_attn_scales_down, L0_attn_lora_A_h, L0_attn_lora_A_down, L0_attn_lora_B_attn, L0_attn_lora_B_gu, L0_attn_lora_B_down, L0_ffn_gate_w, L0_ffn_gate_b, L0_ffn_w1, L0_ffn_b1, L0_ffn_w2, L0_ffn_b2):

    def _L0_attn_ref(x, codes_attn, scales_attn, codes_gu, scales_gu, codes_down, scales_down, lora_A_h, lora_A_down, lora_B_attn, lora_B_gu, lora_B_down):
        import jax, jax.numpy as jnp
        import numpy as np
        NF4 = jnp.array([-1.0, -0.6961928009986877, -0.5250730514526367, -0.39491748809814453, -0.28444138169288635, -0.18477343022823334, -0.09105003625154495, 0.0, 0.07958029955625534, 0.16093020141124725, 0.24611230194568634, 0.33791524171829224, 0.44070982933044434, 0.5626170039176941, 0.7229568362236023, 1.0], dtype=jnp.float32)
        BLOCK = 64

        def _dequant(codes, scales):
            w = NF4[codes]
            O, I = w.shape
            w = w.reshape(O, I // BLOCK, BLOCK) * scales[:, :, None]
            return w.reshape(O, I)

        def _lin_lora(x, W, A, B):
            base = jnp.einsum('bsh,oh->bso', x, W)
            lora = jnp.einsum('bsr,or->bso', jnp.einsum('bsh,rh->bsr', x, A), B)
            return base + lora
        q = _lin_lora(x, _dequant(codes_attn[0], scales_attn[0]), lora_A_h[0], lora_B_attn[0])
        k = _lin_lora(x, _dequant(codes_attn[1], scales_attn[1]), lora_A_h[1], lora_B_attn[1])
        v = _lin_lora(x, _dequant(codes_attn[2], scales_attn[2]), lora_A_h[2], lora_B_attn[2])
        attn = (q + k + v) / 3.0
        o = _lin_lora(attn, _dequant(codes_attn[3], scales_attn[3]), lora_A_h[3], lora_B_attn[3])
        x1 = x + o
        g = _lin_lora(x1, _dequant(codes_gu[0], scales_gu[0]), lora_A_h[4], lora_B_gu[0])
        u = _lin_lora(x1, _dequant(codes_gu[1], scales_gu[1]), lora_A_h[5], lora_B_gu[1])
        h = jax.nn.silu(g) * u
        d = _lin_lora(h, _dequant(codes_down, scales_down), lora_A_down, lora_B_down)
        return x1 + d

    def _L0_ffn_ref(h, gate_w, gate_b, w1, b1, w2, b2):
        import jax, jax.numpy as jnp
        import numpy as np
        B, S, D = (4, 256, 512)
        NUM_EXPERTS, TOP_K = (3, 2)

        def _expert_outputs(h, w1, b1, w2, b2):
            pre = jnp.einsum('bsd,edf->ebsf', h, w1) + b1[:, None, None, :]
            act = jnp.stack([jnp.tanh(pre[0]), jax.nn.gelu(pre[1], approximate=False), jax.nn.silu(pre[2])])
            return jnp.einsum('ebsf,efd->ebsd', act, w2) + b2[:, None, None, :]
        b, s, d = h.shape
        vision_len = int(s * 0.3)
        text_strength = jnp.mean(jnp.abs(h[:, vision_len:, :]), axis=(1, 2), keepdims=True)
        vision_strength = jnp.mean(jnp.abs(h[:, :vision_len, :]), axis=(1, 2), keepdims=True)
        modality_ratio = text_strength / (vision_strength + 1e-08)
        modality_ratio = jnp.broadcast_to(modality_ratio, (b, s, 1))
        router_input = jnp.concatenate([h, modality_ratio], axis=-1)
        gate_logits = router_input @ gate_w + gate_b
        gate_scores = jax.nn.softmax(gate_logits, axis=-1)
        top_val, top_idx = jax.lax.top_k(gate_scores, TOP_K)
        top_val = top_val / (jnp.sum(top_val, axis=-1, keepdims=True) + 1e-08)
        expert_out = _expert_outputs(h, w1, b1, w2, b2)
        moe_out = jnp.zeros_like(h)
        batch_idx = jnp.arange(b)
        for i in range(TOP_K):
            j = top_idx[:, 0, i]
            out_i = expert_out[j, batch_idx]
            moe_out = moe_out + top_val[..., i:i + 1] * out_i
        return moe_out
    x = L0_attn_x
    xn = _layernorm(x, axis=-1)
    s = _L0_attn_ref(xn, L0_attn_codes_attn, L0_attn_scales_attn, L0_attn_codes_gu, L0_attn_scales_gu, L0_attn_codes_down, L0_attn_scales_down, L0_attn_lora_A_h, L0_attn_lora_A_down, L0_attn_lora_B_attn, L0_attn_lora_B_gu, L0_attn_lora_B_down)
    g = _silu(_L0_ffn_ref(xn, L0_ffn_gate_w, L0_ffn_gate_b, L0_ffn_w1, L0_ffn_b1, L0_ffn_w2, L0_ffn_b2))
    x = x + s * g
    return x

_drawn_inputs = setup_inputs


def setup_inputs(seed=0):
    import zlib

    import numpy as np

    out = dict(_drawn_inputs(seed))
    spreads = {'L0_ffn_gate_b': (0.0, 0.1), 'L0_ffn_b1': (0.0, 0.556), 'L0_ffn_b2': (0.0, 0.1)}
    factors = {'L0_attn_scales_attn': 8.0,
     'L0_attn_scales_gu': 8.0,
     'L0_attn_scales_down': 8.0,
     'L0_attn_lora_A_h': 8.0,
     'L0_attn_lora_A_down': 8.0,
     'L0_attn_lora_B_attn': 8.0,
     'L0_attn_lora_B_gu': 8.0,
     'L0_attn_lora_B_down': 8.0}
    for name, (base, spread) in spreads.items():
        noise = np.random.default_rng([zlib.crc32(name.encode()), seed]).standard_normal(out[name].shape)
        drawn = base * np.exp(spread * noise) if base else spread * noise
        out[name] = jnp.asarray(drawn.astype(out[name].dtype))
    for name, factor in factors.items():
        out[name] = (out[name] * factor).astype(out[name].dtype)
    return out
```

```python
from contextlib import ExitStack

import concourse.bass as bass
from concourse import mybir

F32 = mybir.dt.float32
F16 = mybir.dt.float16
I32 = mybir.dt.int32
ALU = mybir.AluOpType
ACT = mybir.ActivationFunctionType

NF4 = [-1.0, -0.6961928009986877, -0.5250730514526367, -0.39491748809814453, -0.28444138169288635,
       -0.18477343022823334, -0.09105003625154495, 0.0, 0.07958029955625534, 0.16093020141124725,
       0.24611230194568634, 0.33791524171829224, 0.44070982933044434, 0.5626170039176941,
       0.7229568362236023, 1.0]

P = 128
B, S, D = 2, 1024, 512
T = B * S
KT = D // P
NST = T // P
CH = 512
NCH = T // CH
SPC = CH // P
I = 1792
UNITS = I // P
R = 16
E = 3
NB = D // 64
PC = 512
WS = 64.0
AS, BS = 16.0, 4.0
EPS = 1e-5
VISION = int(S * 0.3)
GROUPS = [(0, 2), (2, 4), (6, 4), (10, 4)]
SLOTS = 8
ROT = 6


def slot_of(u):
    return (u + ROT) % SLOTS


def nf4_terms():
    v = NF4
    line = [(v[k + 1] - v[k], v[k] - (v[k + 1] - v[k]) * k) for k in range(1, 15, 2)]
    mid = 3
    rights = [(line[n + 1][0] - line[n][0], line[n + 1][1] - line[n][1]) for n in range(mid, 6)]
    lefts = [(line[n][0] - line[n - 1][0], line[n][1] - line[n - 1][1]) for n in range(mid, 0, -1)]
    steep = (v[1] - v[0]) - line[0][0]
    cap_at = 15.0 - ((v[15] - v[14]) - line[6][0]) / steep
    terms = [rights[0], (steep, -steep), lefts[0], rights[1], lefts[1], rights[2], lefts[2]]
    return line[mid][0] + steep, line[mid][1] - steep, steep * (cap_at - 1.0), terms


NF4_SLOPE, NF4_CONST, NF4_CAP, NF4_TERMS = nf4_terms()
NTERM = len(NF4_TERMS)
HR = 4
ADDS = 7
READ_BY = [1, 2, 2, 3, 4, 5, 6]
TERMS_NEEDED = [0, 1, 3, 4, 5, 6, 7, 7]
SUM_BEFORE = [0, 0, 0, 1, 2, 3, 4, 6]


def build(nc, x, attn_codes, attn_scales, attn_scales_o, unit_codes, unit_scales, lora_bt, lora_a,
          lora_a3, lora_bt3, lora_au, lora_bu, lora_ad, lora_bd, gate_w, gate_tail, gate_b, w1, b1, w2, b2,
          eye, region, m_store, out):
    ctx = ExitStack()
    with ctx:
        def sb(name, shape, dt):
            return ctx.enter_context(nc.sbuf_tensor(name, shape, dt))

        def sem(name):
            return ctx.enter_context(nc.semaphore(name))

        reg_a = sb("reg_a", [P, NST * D], F32)
        xnT = reg_a[:, :].bitcast(F16).rearrange("p (h k t) -> p h k t", h=2, k=KT)
        acc = reg_a[:, :].rearrange("p (s d) -> p s d", d=D)
        reg_b = sb("reg_b", [P, NST * D], F32)
        xs = reg_b[:, :].rearrange("p (s d) -> p s d", d=D)
        wpair = reg_b[:, 0:4096].bitcast(F16).rearrange("p (w h k f) -> p w h k f", w=2, h=2, k=KT)
        wstage = reg_b[:, 4096:8192].rearrange("p (w n) -> p w n", w=2)
        x1T = reg_b[:, :].bitcast(F16).rearrange("p (h k t) -> p h k t", h=2, k=KT)
        reg_c = sb("reg_c", [P, SLOTS * 3 * PC], F32)
        units = reg_c[:, :].bitcast(F16).rearrange("p (s h n) -> p s h n", s=SLOTS, h=2)
        mix = reg_c[:, 0:4096].rearrange("p (s d) -> p s d", d=D)
        NRAW = 2 * D + I + 2 * I + D
        raw = reg_c[:, 4096:4096 + NRAW]
        L0 = 4096 + NRAW
        la = reg_c[:, L0:L0 + D]
        lb = reg_c[:, L0 + D:L0 + D + P]
        b2p = reg_c[:, L0 + D + P:L0 + 2 * D + P].bitcast(F16).rearrange("p (s n) -> p s n", s=2)
        assert L0 + 2 * D + P <= SLOTS * 3 * PC
        reg_d = sb("reg_d", [P, 4096], F32)
        hmix = reg_d[:, :].bitcast(F16).rearrange("p (c h f t) -> p c h f t", c=2, h=2, f=KT)
        hffn = reg_d[:, 0:1024].bitcast(F16).rearrange("p (r h t) -> p r h t", r=2, h=2)
        sgate = reg_d[:, 1024:2048].rearrange("p (r t) -> p r t", r=2)
        h32 = reg_d[:, 2048:3072].rearrange("p (r t) -> p r t", r=2)
        act32 = sb("act32", [P, 2, CH], F32)
        reg_e = sb("reg_e", [P, 2 * KT * D], F32)
        wa = reg_e[:, 0:KT * D].rearrange("p (k n) -> p k n", k=KT)
        w3 = reg_e[:, KT * D:2 * KT * D].rearrange("p (k n) -> p k n", k=KT)
        fin_m = reg_e[:, 0:1024].rearrange("p (r d) -> p r d", r=2)
        fin_x = reg_e[:, 1024:2048].rearrange("p (r d) -> p r d", r=2)
        fin_g = reg_e[:, 2048:3072].rearrange("p (r d) -> p r d", r=2)
        fin_t = reg_e[:, 3072:4096].rearrange("p (r d) -> p r d", r=2)
        cpair = sb("cpair", [P, 2, KT, D], F16)
        stack = sb("stack", [P, NRAW], F16)
        s_au = stack[:, 0:2 * D].rearrange("p (g n) -> p g n", g=2)
        s_ad = stack[:, 2 * D:2 * D + I]
        s_bu = stack[:, 2 * D + I:2 * D + 3 * I].rearrange("p (g n) -> p g n", g=2)
        s_bd = stack[:, 2 * D + 3 * I:NRAW]
        codes = sb("codes", [P, 4, PC], I32)
        scl = sb("scl", [P, 3, PC], F32)
        term = sb("term", [P, HR, PC], F32)
        suma = sb("suma", [P, 3, PC], F32)
        sumb = sb("sumb", [P, PC], F32)
        tbias = sb("tbias", [P, 2, NTERM], F32)
        ascl = sb("ascl", [P, KT, 3 * NB], F32)
        b2r = scl[:, 1:3, :]
        ident = sb("ident", [P, P], F32)
        ident3 = sb("ident3", [P, P], F32)
        ident64 = sb("ident64", [P, P], F16)
        ones = sb("ones", [P, P], F32)
        ones16 = sb("ones16", [P, P], F16)
        share = sb("share", [P, NST, 2], F32)
        shared_abs = sb("shared_abs", [P, NST, 2], F32)
        abs_part = sb("abs_part", [P, B, 2], F32)
        bst = sb("bst", [P, NST, 6], F32)
        mv = sb("mv", [P, NST, 2], F32)
        std = sb("std", [P, NST], F32)
        rstd = sb("rstd", [P, NST], F32)
        epst = sb("epst", [P, 1], F32)
        absum = sb("absum", [P, NST], F32)
        gw = sb("gw", [P, KT, E], F32)
        gw6 = sb("gw6", [P, KT, 2 * E], F16)
        gtail = sb("gtail", [P, 2, E], F32)
        strength = sb("strength", [P, B, 2], F32)
        ratio = sb("ratio", [P, B], F32)
        addl = sb("addl", [P, B, E], F32)
        lgt = sb("lgt", [P, NST, E], F32)
        lgs = sb("lgs", [P, NST, E], F32)
        pr = sb("pr", [P, NST, E], F32)
        rt = sb("rt", [P, 8, NST], F32)
        coef = sb("coef", [P, B, 2, NST // B], F32)
        rk = sb("rk", [1, 12, B], F32)
        idx = sb("idx", [1, 8], I32)
        b1t = sb("b1t", [P, 2, KT], F32)

        ps = ctx.enter_context(nc.psum_tensor("ps", [P, 8, 512], F32))
        PRE, OUT, ABA, UBA, GATE, UP, DOWN = 0, 2, 4, 6, 0, 1, 2
        LOGIT, STRENGTH = 6, 7

        x_in = [sem(f"x_in{q}") for q in range(NCH)]
        const_in = sem("const_in")
        raw_zero = sem("raw_zero")
        raw_in = sem("raw_in")
        gp_step = sem("gp_step")
        stacks_ready = sem("stacks_ready")
        setup_done = sem("setup_done")
        ident_ready = sem("ident_ready")
        stats_step = sem("stats_step")
        stats_ready = sem("stats_ready")
        std_ready = sem("std_ready")
        rstd_ready = sem("rstd_ready")
        xn_ready = sem("xn_ready")
        abs_done = sem("abs_done")
        xt_ps = sem("xt_ps")
        xt_hi = sem("xt_hi")
        xt_lo = sem("xt_lo")
        gw_ready = sem("gw_ready")
        logits_ps = sem("logits_ps")
        abs_ready = sem("abs_ready")
        strength_ps = sem("strength_ps")
        rt_step = sem("rt_step")
        lgs_ready = sem("lgs_ready")
        exp_ready = sem("exp_ready")
        idx_ready = sem("idx_ready")
        w_in = [sem(f"w{w + 1}_in") for w in range(2)]
        w_hi = [sem(f"w{w + 1}_hi") for w in range(2)]
        w_ready = [sem(f"w{w + 1}_ready") for w in range(2)]
        b1_in = [sem(f"b1_in{r}") for r in range(2)]
        b2_in = [sem(f"b2_in{r}") for r in range(2)]
        b2_hi = sem("b2_hi")
        b2_ready = sem("b2_ready")
        pre_ps = sem("pre_ps")
        act_ready = sem("act_ready")
        hmix_ready = sem("hmix_ready")
        out_ps = sem("out_ps")
        out0_read = sem("out0_read")
        out1_read = sem("out1_read")
        mix_stored = sem("mix_stored")
        mix_free = sem("mix_free")
        acodes_in = [sem(f"acodes_in{k}") for k in range(4)]
        ascl_in = sem("ascl_in")
        lb_in = sem("lb_in")
        aterm = sem("aterm")
        aread = sem("aread")
        ascaled = sem("ascaled")
        amerged = sem("amerged")
        aba_ps = sem("aba_ps")
        c_ps = sem("c_ps")
        c_hi = sem("c_hi")
        c_ready = sem("c_ready")
        x1_ps = sem("x1_ps")
        x1_hi = sem("x1_hi")
        x1_ready = sem("x1_ready")
        ucodes_in = [sem(f"ucodes_in{k}") for k in range(3)]
        uscl_in = [sem(f"uscl_in{k}") for k in range(3)]
        uterm = sem("uterm")
        uread = sem("uread")
        uscaled = sem("uscaled")
        usum = sem("usum")
        uhi = sem("uhi")
        uready = sem("uready")
        uba_ps = sem("uba_ps")
        gate_ps = sem("gate_ps")
        up_ps = sem("up_ps")
        silu_done = sem("silu_done")
        h_ready32 = sem("h_ready32")
        h_hi = sem("h_hi")
        h_ready = sem("h_ready")
        down_ps = sem("down_ps")
        down_read = sem("down_read")
        fm_in = [sem(f"fm_in{r}") for r in range(2)]
        fx_in = [sem(f"fx_in{r}") for r in range(2)]
        fgate = sem("fgate")
        fprod = sem("fprod")
        fout = sem("fout")
        stored = [sem(f"stored{r}") for r in range(2)]

        block = ctx.enter_context(nc.Block())

        VEC_SEQ, SCA_SEQ = [], []
        for k in range(3):
            VEC_SEQ += [(k, 1), (k, 2)] + ([(k - 1, 10)] if k else []) + [(k, n) for n in range(3, 10)]
            SCA_SEQ += [(k, n) for n in range(4)] + ([(k - 1, 8)] if k else []) + [(k, n) for n in range(4, NTERM)]
        VEC_SEQ += [(2, 10)]
        SCA_SEQ += [(2, 8)]

        def part(seq, i, n):
            return seq[len(seq) * i // n:len(seq) * (i + 1) // n]

        tiles_before = [NCH * sum(n for _, n in GROUPS[:g]) for g in range(len(GROUPS))]

        def col(v, n):
            return slice(v, v + n) if isinstance(v, int) else bass.ds(v, n)

        @block.sync
        def _(sp):
            for q in range(NCH):
                sp.dma_start(xs[:, q * SPC:(q + 1) * SPC, :],
                             x[q * CH:(q + 1) * CH, :].rearrange("(s p) d -> p s d", p=P)).then_inc(x_in[q], 16)
            for dst, src in ((ident[:, :], eye), (share[:, :, :], region), (ascl[:, :, :], attn_scales),
                             (gw[:, :, :], gate_w), (gtail[:, 0, :], gate_tail.to_broadcast([P, E])),
                             (gtail[:, 1, :], gate_b.to_broadcast([P, E])),
                             (la[0:3 * R, :], lora_a), (la[64:64 + R, :], lora_bt3)):
                sp.dma_start(dst, src).then_inc(const_in, 16)
            sp.wait_ge(setup_done, 2)

            def load_attn(n):
                for k in range(4):
                    sp.wait_ge(amerged, 4 * n + k + 1)
                    sp.dma_start(codes[:, k, :],
                                 attn_codes[bass.ds(n, 1), k, :, :].rearrange("a p c -> p (a c)")).then_inc(acodes_in[k], 16)
                sp.dma_start(lb[0:3 * R, :], lora_bt[bass.ds(n, 1), :, :].rearrange("a r m -> r (a m)")).then_inc(lb_in, 16)
                sp.dma_start(lb[64:64 + R, :], lora_a3[bass.ds(n, 1), :, :].rearrange("a r m -> r (a m)")).then_inc(lb_in, 16)
                for half in range(2):
                    sp.dma_start(scl[64 * half:64 * half + 64, 0, :],
                                 attn_scales_o[bass.ds(n, 1), half, :].to_broadcast([64, PC])).then_inc(ascl_in, 16)

            def load_w(n, w, slot):
                j = sp.value_load(idx[0:1, col(n, 1)], min_val=0, max_val=E - 1)
                sp.wait_ge(w_ready[w], n + 1)
                if w == 0:
                    sp.dma_start(b1t[:, slot, :], b1[bass.ds(j, 1), :, :].rearrange("a p k -> p (a k)")).then_inc(b1_in[slot], 16)
                else:
                    for row in (0, 32):
                        sp.dma_start(b2r[row:row + 1, slot, :], b2[bass.ds(j, 1), :]).then_inc(b2_in[slot], 16)
                sp.dma_start(wstage[:, w, :].rearrange("p (k f) -> p k f", k=KT),
                             (w1, w2)[w][bass.ds(j, 1), :, :].rearrange("a (k p) f -> p (a k) f", p=P)).then_inc(w_in[w], 16)

            sp.wait_ge(idx_ready, 1)
            sp.wait_ge(xt_lo, NST)
            sp.wait_ge(abs_done, NST + 2)
            with sp.Fori(0, B) as b:
                for slot in range(2):
                    load_w(2 * b + slot, 0, slot)
                    load_w(2 * b + slot, 1, slot)
                    load_attn(2 * b + slot)
            load_w(2 * B, 0, 0)

            sp.wait_ge(amerged, 4 * 4 + 4)
            sp.wait_ge(b2_ready, 2 * B)
            with sp.Fori(0, UNITS) as u:
                for k in range(3):
                    sp.wait_ge(usum, 3 * u + k + 1)
                    sp.dma_start(codes[:, k, :],
                                 unit_codes[bass.ds(u, 1), k, :, :].rearrange("a p c -> p (a c)")).then_inc(ucodes_in[k], 16)
                    for half in range(2):
                        sp.dma_start(scl[64 * half:64 * half + 64, k, :],
                                     unit_scales[bass.ds(u, 1), k, half, :].to_broadcast([64, PC])).then_inc(uscl_in[k], 16)

        @block.gpsimd
        def _(gp):
            nc.gpsimd.memset(raw, 0.0).then_inc(raw_zero, 1)
            gp.wait_ge(raw_zero, 1)
            for q in range(4):
                r0 = 32 * q
                for dst, src in ((raw[r0:r0 + R, 0:2 * D], lora_au), (raw[r0:r0 + R, 2 * D:2 * D + I], lora_ad),
                                 (raw[r0:r0 + R, 2 * D + I:2 * D + 3 * I], lora_bu),
                                 (raw[r0:r0 + R, 2 * D + 3 * I:NRAW], lora_bd)):
                    gp.dma_start(dst, src).then_inc(raw_in, 16)
            gp.wait_ge(raw_in, 16 * 16)
            na = 2 * D + I
            nc.gpsimd.tensor_scalar(raw[:, 0:na], raw[:, 0:na], AS, 0.0, ALU.mult, ALU.add).then_inc(gp_step, 1)
            nc.gpsimd.tensor_scalar(raw[:, na:NRAW], raw[:, na:NRAW], BS, 0.0, ALU.mult, ALU.add).then_inc(gp_step, 1)
            gp.wait_ge(gp_step, 2)
            nc.gpsimd.tensor_copy(stack[:, :], raw).then_inc(gp_step, 1)
            gp.wait_ge(gp_step, 3)
            for done, (p0, n, c0, c1) in enumerate(((64, 64, 0, na), (32, 32, na, NRAW), (96, 32, na, NRAW))):
                if done:
                    gp.wait_ge(stacks_ready, done)
                nc.gpsimd.tensor_tensor(stack[p0:p0 + n, c0:c1], raw[p0:p0 + n, c0:c1], stack[p0:p0 + n, c0:c1],
                                        ALU.subtract).then_inc(stacks_ready, 1)
            gp.sem_inc(mix_free, 1)
            with gp.Fori(0, B) as b:
                gp.wait_ge(out1_read, 8 * b + 16)
                gp.dma_start(m_store[bass.ds(b, 1), :, :, :].rearrange("a s p d -> p (a s) d"), mix).then_inc(mix_stored, 16)
                gp.wait_ge(mix_stored, 16 * b + 16)
                gp.sem_inc(mix_free, 1)

            gp.wait_ge(c_ready, KT)
            gp.sem_inc(fout, 2)
            tiles = "(s p) d -> s p d"

            def load_fin(t, r):
                gp.dma_start(fin_m[:, r, :], m_store.rearrange("b s p d -> (b s) p d")[col(t, 1), :, :].rearrange("a p d -> p (a d)")).then_inc(fm_in[r], 16)
                gp.dma_start(fin_x[:, r, :], x.rearrange(tiles, p=P)[col(t, 1), :, :].rearrange("a p d -> p (a d)")).then_inc(fx_in[r], 16)

            def add_store(i, r):
                t = 2 * i + r
                gp.wait_ge(fprod, t + 3)
                gp.wait_ge(fx_in[r], 16 * i + 16)
                nc.gpsimd.tensor_tensor(fin_x[:, r, :], fin_t[:, r, :], fin_x[:, r, :], ALU.add).then_inc(fout, 1)
                gp.wait_ge(fout, t + 3)
                gp.dma_start(out.rearrange(tiles, p=P)[col(t, 1), :, :].rearrange("a p d -> p (a d)"), fin_x[:, r, :]).then_inc(stored[r], 16)

            load_fin(0, 0)
            load_fin(1, 1)
            with gp.Fori(0, NST // 2 - 1) as i:
                for r in range(2):
                    add_store(i, r)
                    gp.wait_ge(stored[r], 16 * i + 16)
                    load_fin(2 * i + r + 2, r)
            for r in range(2):
                add_store(NST // 2 - 1, r)
            for r in range(2):
                gp.wait_ge(stored[r], 16 * (NST // 2))

        @block.scalar
        def _(act):
            act.wait_ge(setup_done, 2)
            act.sem_inc(abs_done, 2)
            for b in range(B):
                s0 = b * NST // B
                act.wait_ge(stats_ready, (b + 1) * NST // B)
                nc.scalar.activation(std[:, s0:s0 + NST // B], mv[:, s0:s0 + NST // B, 1], ACT.Sqrt,
                                     bias=epst[:, 0:1]).then_inc(std_ready, 1)
            with act.Fori(0, NST // 2) as i:
                for r in range(2):
                    t = 2 * i + r
                    act.wait_ge(xt_ps, t + 1)
                    nc.scalar.activation(xnT[:, 0, :, bass.ds(t * P, P)],
                                         ps[:, r, :].rearrange("p (k t) -> p k t", k=KT), ACT.Copy).then_inc(xt_hi, 1)
                    act.wait_ge(abs_done, t + 1)
                    nc.scalar.activation(term[:, r, :], xs[:, bass.ds(t, 1), :].rearrange("p a d -> p (a d)"), ACT.Abs,
                                         accum_out=absum[:, bass.ds(t, 1)]).then_inc(abs_done, 1)
            act.wait_ge(lgs_ready, 1)
            nc.scalar.activation(pr[:, :, :], lgs[:, :, :], ACT.Exp).then_inc(exp_ready, 1)

            def nf4_term(e, codes_k, ws, done):
                nc.scalar.activation(term[:, e % HR, :], codes_k, ACT.Relu, bias=tbias[:, ws, e:e + 1],
                                     scale=NF4_TERMS[e][0] * (WS if ws else 1.0)).then_inc(done, 1)

            def term_free(e):
                if e >= HR:
                    return READ_BY[e - HR] + ADDS
                return READ_BY[e + HR if e + HR < NTERM else e]

            def attn_term(n, k, e):
                if e == 0:
                    act.wait_ge(acodes_in[k], 16 * n + 16)
                act.wait_ge(aread, ADDS * (4 * n + k) + term_free(e))
                nf4_term(e, codes[:, k, :], 0, aterm)

            def w_high(w):
                nc.scalar.activation(wpair[:, w, 0, :, :], wstage[:, w, :].rearrange("p (k f) -> p k f", k=KT),
                                     ACT.Copy, scale=WS).then_inc(w_hi[w], 1)

            act.sem_inc(act_ready, 2)
            act.wait_ge(w_in[0], 16)
            w_high(0)
            with act.Fori(0, B) as b:
                for slot in range(2):
                    n = 2 * b + slot
                    j = act.value_load(idx[0:1, bass.ds(n, 1)], min_val=0, max_val=E - 1)
                    for expert, func in ((0, ACT.Tanh), (1, ACT.Gelu), (2, ACT.Silu)):
                        with act.If(j == expert):
                            act.wait_ge(b1_in[slot], 16 * b + 16)
                            for t in range(2 * KT):
                                c, f = t // KT, t % KT
                                act.wait_ge(pre_ps, 8 * n + t + 1)
                                act.wait_ge(hmix_ready, 8 * n + t + 1)
                                nc.scalar.activation(act32[:, t % 2, :], ps[:, PRE + t % 2, :], func,
                                                     bias=b1t[:, slot, f:f + 1], scale=1.0 / WS)
                                nc.scalar.activation(hmix[:, c, 0, f, :], ps[:, PRE + t % 2, :], func,
                                                     bias=b1t[:, slot, f:f + 1], scale=1.0 / WS).then_inc(act_ready, 1)
                                if t == 0:
                                    act.wait_ge(w_in[1], 16 * n + 16)
                                    w_high(1)
                                for e in part(range(NTERM), t % 4, 4):
                                    attn_term(n, t // 4, e)
                    act.wait_ge(w_in[0], 16 * n + 32)
                    w_high(0)
                    for s in range(8):
                        if slot == 0:
                            if s == 0:
                                act.wait_ge(mix_free, b + 1)
                            act.wait_ge(out_ps, 8 * n + s + 1)
                            nc.scalar.activation(mix[:, s, :], ps[:, OUT + s % 2, :], ACT.Copy,
                                                 scale=coef[:, bass.ds(b, 1), 0, s]).then_inc(out0_read, 1)
                        for e in part(range(NTERM), s % 4, 4):
                            attn_term(n, 2 + s // 4, e)

            for k in range(KT):
                act.wait_ge(c_ps, k + 1)
                nc.scalar.activation(cpair[:, 0, k, :], ps[:, k, :], ACT.Copy, scale=WS / 3.0).then_inc(c_hi, 1)

            def unit_step(u, slot, k, e):
                p = 3 * u + k
                if e == 8:
                    act.wait_ge(usum, p + 4)
                    nc.scalar.activation(units[:, col(slot, 1), 0, k * PC:(k + 1) * PC].rearrange("p a n -> p (a n)"),
                                         suma[:, k, :], ACT.Copy).then_inc(uhi, 1)
                    return
                if e == 0:
                    act.wait_ge(ucodes_in[k], 16 * u + 16)
                act.wait_ge(uread, ADDS * p + term_free(e))
                nf4_term(e, codes[:, k, :], 1, uterm)

            with act.Fori(0, 2) as i:
                for t in range(8):
                    c, o = t // KT, t % KT
                    act.wait_ge(x1_ps, 8 * i + t + 1)
                    nc.scalar.activation(x1T[:, 0, o, bass.ds(i * (2 * CH) + c * CH, CH)], ps[:, t % 4, :], ACT.Copy,
                                         scale=1.0 / WS).then_inc(x1_hi, 1)
                    for k, e in part(SCA_SEQ, t, 8):
                        unit_step(i, i + slot_of(0), k, e)

            def silu(q, r):
                act.wait_ge(gate_ps, q + 1)
                nc.scalar.activation(sgate[:, r, :], ps[:, GATE, :], ACT.Silu, scale=1.0 / WS).then_inc(silu_done, 1)

            def high(q, r):
                act.wait_ge(h_ready32, q + 1)
                nc.scalar.activation(hffn[:, r, 0, :], h32[:, r, :], ACT.Copy).then_inc(h_hi, 1)

            def body(g, c, last):
                first, n = GROUPS[g]
                q = tiles_before[g] + c * n
                new = GROUPS[g + 1][0] if g + 1 < len(GROUPS) else None
                for v in range(1, n + 1):
                    steps = part(SCA_SEQ, v - 1, n) if new is not None else []
                    if not (last and v == n):
                        silu(q + v, v % 2)
                    for k, e in steps[:2]:
                        unit_step(new + c, slot_of(new) + c, k, e)
                    if not (last and v == n):
                        high(q + v, v % 2)
                    for k, e in steps[2:]:
                        unit_step(new + c, slot_of(new) + c, k, e)
                if new is None:
                    for s in range(SPC):
                        t, r = SPC * c + s, s % 2
                        act.wait_ge(fm_in[r], 16 * (2 * c + s // 2) + 16)
                        act.wait_ge(fprod, t + 1)
                        nc.scalar.activation(fin_g[:, r, :], fin_m[:, r, :], ACT.Silu).then_inc(fgate, 1)

            act.wait_ge(mix_free, B + 1)
            silu(0, 0)
            high(0, 0)
            for g in range(len(GROUPS)):
                with act.Fori(0, NCH - 1) as c:
                    body(g, c, False)
                body(g, NCH - 1, g == len(GROUPS) - 1)

        @block.vector
        def _(vec):
            vector = nc.vector
            for e, (_, bias) in enumerate(NF4_TERMS):
                vector.memset(tbias[:, 0, e:e + 1], bias)
                vector.memset(tbias[:, 1, e:e + 1], bias * WS)
            vector.memset(epst[:, :], EPS)
            vector.memset(ones[:, :], 1.0)
            vector.memset(ones16[:, :], 1.0).then_inc(setup_done, 1)
            vector.memset(idx[:, :], 0)
            vector.memset(b2r, 0.0).then_inc(setup_done, 1)
            vec.sem_inc(hmix_ready, 2)
            vec.sem_inc(out1_read, 8)
            vec.sem_inc(aread, ADDS)
            vec.sem_inc(amerged, 4)
            vec.sem_inc(uread, ADDS)
            vec.sem_inc(usum, 3)
            vec.sem_inc(x1_ready, 4)
            vec.sem_inc(down_read, 4)
            vec.sem_inc(fprod, 2)
            for w in range(2):
                vec.sem_inc(w_ready[w], 1)

            for b in range(B):
                for q in range(b * NCH // B, (b + 1) * NCH // B):
                    vec.wait_ge(x_in[q], 16)
                    for t in range(q * SPC, (q + 1) * SPC):
                        vector.bn_stats(bst[:, t, :], xs[:, t, :]).then_inc(stats_step, 1)
                    for t in range(q * SPC, (q + 1) * SPC):
                        vec.wait_ge(stats_step, t + 1)
                        vector.bn_aggr(mv[:, t, :], bst[:, t, :]).then_inc(stats_ready, 1)
                if b == 0:
                    vec.wait_ge(const_in, 16 * 8)
                    vector.tensor_scalar(ident3[:, :], ident[:, :], 3.0, None, ALU.mult)
                    vector.tensor_scalar(ident64[:, :], ident[:, :], WS, None, ALU.mult).then_inc(ident_ready, 1)
                    vector.tensor_scalar(gw6[:, :, 0:E], gw[:, :, :], WS, None, ALU.mult).then_inc(gw_ready, 1)
                    vec.wait_ge(gw_ready, 1)
                    vector.scalar_tensor_tensor(gw6[:, :, E:2 * E], gw[:, :, :], WS, gw6[:, :, 0:E], ALU.mult,
                                                ALU.subtract).then_inc(gw_ready, 1)
                vec.wait_ge(std_ready, b + 1)
                t0, t1 = b * NST // B, (b + 1) * NST // B
                vector.reciprocal(rstd[:, t0:t1], std[:, t0:t1]).then_inc(rstd_ready, 1)
                vec.wait_ge(rstd_ready, b + 1)
                for t in range(t0, t1):
                    vector.tensor_scalar(xs[:, t, :], xs[:, t, :], mv[:, t, 0:1], rstd[:, t:t + 1], ALU.subtract,
                                         ALU.mult).then_inc(xn_ready, 1)
            with vec.Fori(0, NST // 2) as i:
                for r in range(2):
                    t = 2 * i + r
                    vec.wait_ge(xt_hi, t + 1)
                    vector.tensor_tensor(xnT[:, 1, :, bass.ds(t * P, P)], ps[:, r, :].rearrange("p (k t) -> p k t", k=KT),
                                         xnT[:, 0, :, bass.ds(t * P, P)], ALU.subtract).then_inc(xt_lo, 1)

            linked = [0]

            def link(ins):
                linked[0] += 1
                ins.then_inc(rt_step, 1)
                vec.wait_ge(rt_step, linked[0])

            vec.wait_ge(abs_done, NST + 2)
            link(vector.tensor_tensor(shared_abs[:, :, :], share[:, :, :], absum[:, :].unsqueeze(2).to_broadcast([P, NST, 2]), ALU.mult))
            vector.tensor_reduce(abs_part[:, :, :], shared_abs[:, :, :].rearrange("p (b s) r -> p b r s", b=B),
                                 mybir.AxisListType.X, ALU.add).then_inc(abs_ready, 1)
            vec.wait_ge(strength_ps, 1)
            link(vector.tensor_copy(strength[:, :, :], ps[:, STRENGTH, 0:2 * B].rearrange("p (b r) -> p b r", b=B)))
            link(vector.tensor_scalar(ratio[:, :], strength[:, :, 1], 1e-8, None, ALU.add))
            link(vector.reciprocal(ratio[:, :], ratio[:, :]))
            link(vector.tensor_tensor(ratio[:, :], ratio[:, :], strength[:, :, 0], ALU.mult))
            for b in range(B):
                link(vector.scalar_tensor_tensor(addl[:, b, :], gtail[:, 0, :], ratio[:, b:b + 1], gtail[:, 1, :], ALU.mult, ALU.add))
            vec.wait_ge(logits_ps, NST)
            raw_logits = ps[:, LOGIT, 0:2 * E * NST].rearrange("p (t e) -> p t e", e=2 * E)
            link(vector.tensor_copy(lgs[:, :, :], raw_logits[:, :, E:2 * E]))
            link(vector.tensor_tensor(lgt[:, :, :], raw_logits[:, :, 0:E], lgs[:, :, :], ALU.add))
            for b in range(B):
                t0, t1 = b * NST // B, (b + 1) * NST // B
                link(vector.scalar_tensor_tensor(lgt[:, t0:t1, :], lgt[:, t0:t1, :], 1.0 / WS,
                                                 addl[:, b:b + 1, :].to_broadcast([P, NST // B, E]), ALU.mult, ALU.add))
            link(vector.tensor_tensor(rt[:, 0, :], lgt[:, :, 0], lgt[:, :, 1], ALU.max))
            link(vector.tensor_tensor(rt[:, 0, :], rt[:, 0, :], lgt[:, :, 2], ALU.max))
            vector.tensor_tensor(lgs[:, :, :], lgt[:, :, :], rt[:, 0, :].unsqueeze(2).to_broadcast([P, NST, E]),
                                 ALU.subtract).then_inc(lgs_ready, 1)
            vec.wait_ge(exp_ready, 1)
            link(vector.tensor_tensor(rt[:, 1, :], pr[:, :, 0], pr[:, :, 1], ALU.add))
            link(vector.tensor_tensor(rt[:, 1, :], rt[:, 1, :], pr[:, :, 2], ALU.add))
            link(vector.reciprocal(rt[:, 1, :], rt[:, 1, :]))
            link(vector.tensor_tensor(pr[:, :, :], pr[:, :, :], rt[:, 1, :].unsqueeze(2).to_broadcast([P, NST, E]), ALU.mult))
            p0t = [pr[0:1, :, :].rearrange("p (b s) e -> p b s e", b=B)[:, :, 0, e] for e in range(E)]
            for row, a, b_, op in ((0, 1, 0, ALU.is_gt), (1, 2, 0, ALU.is_gt), (2, 0, 1, ALU.is_ge),
                                   (3, 2, 1, ALU.is_gt), (4, 0, 2, ALU.is_ge), (5, 1, 2, ALU.is_ge)):
                last = vector.tensor_tensor(rk[:, row, :], p0t[a], p0t[b_], op)
            link(last)
            for e in (1, 2):
                last = vector.tensor_tensor(rk[:, 6 + e, :], rk[:, 2 * e, :], rk[:, 2 * e + 1, :], ALU.add)
            link(last)
            for choice in range(2):
                vector.tensor_scalar(rk[:, 9, :], rk[:, 7, :], float(choice), None, ALU.is_equal)
                link(vector.tensor_scalar(rk[:, 10, :], rk[:, 8, :], float(choice), 2.0, ALU.is_equal, ALU.mult))
                link(vector.tensor_tensor(rk[:, 11, :], rk[:, 9, :], rk[:, 10, :], ALU.add))
                last = vector.tensor_scalar(idx[:, 0:2 * B].rearrange("p (b c) -> p b c", b=B)[:, :, choice],
                                            rk[:, 11, :], float(E - 1), None, ALU.min)
            last.then_inc(idx_ready, 1)
            last = vector.tensor_tensor(rt[:, 2, :], pr[:, :, 0], pr[:, :, 1], ALU.max)
            link(vector.tensor_tensor(rt[:, 3, :], pr[:, :, 0], pr[:, :, 1], ALU.min))
            vector.tensor_tensor(rt[:, 4, :], rt[:, 2, :], pr[:, :, 2], ALU.max)
            link(vector.tensor_tensor(rt[:, 5, :], rt[:, 2, :], pr[:, :, 2], ALU.min))
            link(vector.tensor_tensor(rt[:, 5, :], rt[:, 5, :], rt[:, 3, :], ALU.max))
            link(vector.tensor_tensor(rt[:, 6, :], rt[:, 4, :], rt[:, 5, :], ALU.add))
            link(vector.tensor_scalar(rt[:, 6, :], rt[:, 6, :], 1e-8, None, ALU.add))
            link(vector.reciprocal(rt[:, 6, :], rt[:, 6, :]))
            for choice in range(2):
                link(vector.scalar_tensor_tensor(coef[:, :, choice, :], rt[:, 4 + choice, :].rearrange("p (b s) -> p b s", b=B),
                                                 1.0 / WS, rt[:, 6, :].rearrange("p (b s) -> p b s", b=B), ALU.mult, ALU.mult))

            def addition(k, step, codes_k, ws, done):
                a, b_ = suma[:, k, :], sumb[:, :]
                if step == 1:
                    ins = vector.scalar_tensor_tensor(a, codes_k, NF4_SLOPE * (WS if ws else 1.0), term[:, 0, :],
                                                      ALU.mult, ALU.add)
                elif step == 2:
                    ins = vector.scalar_tensor_tensor(b_, term[:, 1, :], NF4_CAP * (WS if ws else 1.0), term[:, 2, :],
                                                      ALU.min, ALU.add)
                elif step < 7:
                    s = a if step % 2 else b_
                    ins = vector.tensor_tensor(s, s, term[:, step % HR, :], ALU.add)
                else:
                    ins = vector.tensor_tensor(a, a, b_, ALU.subtract)
                ins.then_inc(done, 1)

            def attn_step(n, k, step):
                p = 4 * n + k
                if step <= ADDS:
                    vec.wait_ge(aterm, NTERM * p + TERMS_NEEDED[step])
                    if step > 2:
                        vec.wait_ge(aread, ADDS * p + ADDS + SUM_BEFORE[step])
                    addition(k % 3, step, codes[:, k, :], 0, aread)
                    return
                blocks = "p (b c) -> p b c"
                target = (wa if k < 3 else w3)[:, col(n, 1), :].rearrange("p a d -> p (a d)")
                mine = suma[:, k % 3, :]
                if step == 8:
                    vec.wait_ge(aread, ADDS * p + 2 * ADDS)
                    dst = target if k in (0, 3) else mine
                    if k == 3:
                        vec.wait_ge(ascl_in, 32 * n + 32)
                        vector.scalar_tensor_tensor(dst, mine, NF4_CONST, scl[:, 0, :], ALU.add, ALU.mult).then_inc(ascaled, 1)
                    else:
                        scales = ascl[:, col(n, 1), k * NB:(k + 1) * NB].rearrange("p a b -> p (a b)")
                        vector.scalar_tensor_tensor(dst.rearrange(blocks, b=NB), mine.rearrange(blocks, b=NB), NF4_CONST,
                                                    scales.unsqueeze(2).to_broadcast([P, NB, D // NB]), ALU.add,
                                                    ALU.mult).then_inc(ascaled, 1)
                else:
                    vec.wait_ge(ascaled, p + 1)
                    vec.wait_ge(amerged, p + 4)
                    if k in (0, 3):
                        vec.wait_ge(aba_ps, 2 * n + (1 if k == 0 else 2))
                        other = ps[:, ABA + (k == 3), :]
                    else:
                        other = mine
                    vector.tensor_tensor(target, other, target, ALU.add).then_inc(amerged, 1)

            ATTN_EVENT = [[(-1, 8), (0, 1)], [(-1, 9), (0, 2)], [(0, 3), (0, 4)], [(0, 5), (0, 6), (0, 7)]]

            def w_low(n, w):
                vec.wait_ge(w_hi[w], n + 1)
                vector.scalar_tensor_tensor(wpair[:, w, 1, :, :].rearrange("p k f -> p (k f)"), wstage[:, w, :], WS,
                                            wpair[:, w, 0, :, :].rearrange("p k f -> p (k f)"), ALU.mult,
                                            ALU.subtract).then_inc(w_ready[w], 1)

            w_low(0, 0)
            with vec.Fori(0, B) as b:
                for slot in range(2):
                    n = 2 * b + slot
                    for t in range(2 * KT):
                        c, f = t // KT, t % KT
                        vec.wait_ge(act_ready, 8 * n + t + 3)
                        vector.tensor_tensor(hmix[:, c, 1, f, :], act32[:, t % 2, :], hmix[:, c, 0, f, :],
                                             ALU.subtract).then_inc(hmix_ready, 1)
                        if t == 0:
                            w_low(n, 1)
                            vec.wait_ge(b2_in[slot], 32 * b + 32)
                            vector.tensor_scalar(b2p[0:33, slot, :], b2r[0:33, slot, :], WS, None, ALU.mult).then_inc(b2_hi, 1)
                            vec.wait_ge(b2_hi, n + 1)
                            vector.scalar_tensor_tensor(b2p[32:33, slot, :], b2r[32:33, slot, :], WS, b2p[32:33, slot, :],
                                                        ALU.mult, ALU.subtract).then_inc(b2_ready, 1)
                        for dk, step in ATTN_EVENT[t % 4]:
                            if t // 4 + dk >= 0:
                                attn_step(n, t // 4 + dk, step)
                    w_low(n + 1, 0)
                    for s in range(8):
                        if slot == 1:
                            vec.wait_ge(out_ps, 8 * n + s + 1)
                            if s == 0:
                                vec.wait_ge(out0_read, 8 * b + 8)
                            vector.scalar_tensor_tensor(mix[:, s, :], ps[:, OUT + s % 2, :], coef[:, bass.ds(b, 1), 1, s],
                                                        mix[:, s, :], ALU.mult, ALU.add).then_inc(out1_read, 1)
                        for dk, step in ATTN_EVENT[s % 4]:
                            attn_step(n, 2 + s // 4 + dk, step)
                    attn_step(n, 3, 8)
                    attn_step(n, 3, 9)

            for k in range(KT):
                vec.wait_ge(c_hi, k + 1)
                vector.scalar_tensor_tensor(cpair[:, 1, k, :], ps[:, k, :], WS / 3.0, cpair[:, 0, k, :], ALU.mult,
                                            ALU.subtract).then_inc(c_ready, 1)

            def unit_step(u, slot, k, step):
                p = 3 * u + k
                if step <= ADDS:
                    vec.wait_ge(uterm, NTERM * p + TERMS_NEEDED[step])
                    if step > 2:
                        vec.wait_ge(uread, ADDS * p + ADDS + SUM_BEFORE[step])
                    addition(k, step, codes[:, k, :], 1, uread)
                elif step == 8:
                    vec.wait_ge(uread, ADDS * p + 2 * ADDS)
                    vec.wait_ge(uscl_in[k], 32 * u + 32)
                    vector.scalar_tensor_tensor(suma[:, k, :], suma[:, k, :], NF4_CONST * WS, scl[:, k, :], ALU.add,
                                                ALU.mult).then_inc(uscaled, 1)
                elif step == 9:
                    vec.wait_ge(uscaled, p + 1)
                    vec.wait_ge(uba_ps, p + 1)
                    vector.tensor_tensor(suma[:, k, :], ps[:, UBA + k % 2, :], suma[:, k, :], ALU.add).then_inc(usum, 1)
                else:
                    vec.wait_ge(uhi, p + 1)
                    high = units[:, col(slot, 1), 0, k * PC:(k + 1) * PC].rearrange("p a n -> p (a n)")
                    low = units[:, col(slot, 1), 1, k * PC:(k + 1) * PC].rearrange("p a n -> p (a n)")
                    vector.tensor_tensor(low, suma[:, k, :], high, ALU.subtract).then_inc(uready, 1)

            with vec.Fori(0, 2) as i:
                for t in range(8):
                    c, o = t // KT, t % KT
                    vec.wait_ge(x1_hi, 8 * i + t + 1)
                    cols = bass.ds(i * (2 * CH) + c * CH, CH)
                    vector.scalar_tensor_tensor(x1T[:, 1, o, cols], ps[:, t % 4, :], 1.0 / WS, x1T[:, 0, o, cols],
                                                ALU.mult, ALU.subtract).then_inc(x1_ready, 1)
                    for k, step in part(VEC_SEQ, t, 8):
                        unit_step(i, i + slot_of(0), k, step)

            def hidden(q, r):
                vec.wait_ge(up_ps, q + 1)
                vec.wait_ge(silu_done, q + 1)
                vector.scalar_tensor_tensor(h32[:, r, :], ps[:, UP, :], 1.0 / WS, sgate[:, r, :], ALU.mult,
                                            ALU.mult).then_inc(h_ready32, 1)

            def low(q, r):
                vec.wait_ge(h_hi, q + 1)
                vector.tensor_tensor(hffn[:, r, 1, :], h32[:, r, :], hffn[:, r, 0, :], ALU.subtract).then_inc(h_ready, 1)

            def body(g, c, last):
                first, n = GROUPS[g]
                q = tiles_before[g] + c * n
                it = NCH * g + c
                new = GROUPS[g + 1][0] if g + 1 < len(GROUPS) else None
                for v in range(1, n + 1):
                    steps = part(VEC_SEQ, v - 1, n) if new is not None else []
                    if not (last and v == n):
                        hidden(q + v, v % 2)
                    for k, step in steps[:2]:
                        unit_step(new + c, slot_of(new) + c, k, step)
                    if not (last and v == n):
                        low(q + v, v % 2)
                    for k, step in steps[2:]:
                        unit_step(new + c, slot_of(new) + c, k, step)
                for s in range(SPC):
                    vec.wait_ge(down_ps, SPC * it + s + 1)
                    mine = acc[:, col(SPC * c + s, 1), :].rearrange("p a d -> p (a d)")
                    if g == 0:
                        vector.tensor_copy(mine, ps[:, DOWN + s, :]).then_inc(down_read, 1)
                    else:
                        vector.tensor_tensor(mine, ps[:, DOWN + s, :], mine, ALU.add).then_inc(down_read, 1)
                if new is None:
                    for s in range(SPC):
                        t, r = SPC * c + s, s % 2
                        vec.wait_ge(down_read, SPC * it + s + 5)
                        vec.wait_ge(fgate, t + 1)
                        vec.wait_ge(fout, t + 1)
                        mine = acc[:, col(t, 1), :].rearrange("p a d -> p (a d)")
                        vector.scalar_tensor_tensor(fin_t[:, r, :], mine, 1.0 / WS, fin_g[:, r, :], ALU.mult,
                                                    ALU.mult).then_inc(fprod, 1)

            hidden(0, 0)
            low(0, 0)
            for g in range(len(GROUPS)):
                with vec.Fori(0, NCH - 1) as c:
                    body(g, c, False)
                body(g, NCH - 1, g == len(GROUPS) - 1)

        @block.tensor
        def _(pe):
            mm = nc.tensor.matmul

            def three(dst, stationary, moving, first, last):
                mm(dst, stationary(0), moving(0), start=first, stop=False)
                mm(dst, stationary(0), moving(1), start=False, stop=False)
                return mm(dst, stationary(1), moving(0), start=False, stop=last)

            pe.wait_ge(const_in, 16 * 8)
            for t in range(NST):
                pe.wait_ge(xn_ready, t + 1)
                if t >= 2:
                    pe.wait_ge(xt_lo, t - 1)
                for k in range(KT):
                    last = nc.tensor.transpose(ps[:, t % 2, k * P:(k + 1) * P], xs[:, t, k * P:(k + 1) * P], ident[:, :])
                last.then_inc(xt_ps, 1)
            pe.wait_ge(gw_ready, 2)
            with pe.Fori(0, NST) as t:
                pe.wait_ge(xt_lo, t + 1)
                for k in range(KT):
                    for h in range(2):
                        last = mm(ps[:, LOGIT, bass.ds(t * (2 * E), 2 * E)], xnT[:, h, k, bass.ds(t * P, P)], gw6[:, k, :],
                                  start=(k == 0 and h == 0), stop=(k == KT - 1 and h == 1))
                last.then_inc(logits_ps, 1)
            pe.wait_ge(abs_ready, 1)
            mm(ps[:, STRENGTH, 0:2 * B], ones[:, :], abs_part[:, :, :].rearrange("p b r -> p (b r)"), start=True,
               stop=True).then_inc(strength_ps, 1)

            with pe.Fori(0, B) as b:
                for slot in range(2):
                    n = 2 * b + slot
                    pe.wait_ge(w_ready[0], n + 2)
                    for t in range(2 * KT):
                        c, f = t // KT, t % KT
                        pe.wait_ge(act_ready, 8 * n + t + 1)
                        for k in range(KT):
                            last = three(ps[:, PRE + t % 2, :], lambda h: wpair[:, 0, h, k, f * P:(f + 1) * P],
                                         lambda h: xnT[:, h, k, bass.ds(b * S + c * CH, CH)], k == 0, k == KT - 1)
                        last.then_inc(pre_ps, 1)
                        if t == 2:
                            pe.wait_ge(lb_in, 32 * n + 32)
                            pe.wait_ge(amerged, 4 * n + 4)
                            mm(ps[:, ABA, :], lb[0:3 * R, :], la[0:3 * R, :], start=True, stop=True).then_inc(aba_ps, 1)
                            mm(ps[:, ABA + 1, :], lb[64:64 + R, :], la[64:64 + R, :], start=True, stop=True).then_inc(aba_ps, 1)
                    pe.wait_ge(w_ready[1], n + 2)
                    pe.wait_ge(b2_ready, n + 1)
                    for s in range(8):
                        c = s // SPC
                        if slot == 0:
                            if s < 2:
                                pe.wait_ge(out1_read, 8 * b + 7 + s)
                            else:
                                pe.wait_ge(out0_read, 8 * b + s - 1)
                        elif s < 2:
                            pe.wait_ge(out0_read, 8 * b + 7 + s)
                        else:
                            pe.wait_ge(out1_read, 8 * b + 7 + s)
                        pe.wait_ge(hmix_ready, 8 * n + 4 * c + 6)
                        mm(ps[:, OUT + s % 2, :], ones16[0:33, :], b2p[0:33, slot, :], start=True, stop=False)
                        tok = slice((s % SPC) * P, (s % SPC + 1) * P)
                        for f in range(KT):
                            last = three(ps[:, OUT + s % 2, :], lambda h: hmix[:, c, h, f, tok],
                                         lambda h: wpair[:, 1, h, f, :], False, f == KT - 1)
                        last.then_inc(out_ps, 1)

            pe.wait_ge(ident_ready, 1)
            pe.wait_ge(amerged, 4 * 4 + 4)
            pe.wait_ge(act_ready, 8 * 4 + 2)
            pe.wait_ge(out1_read, 8 * B + 8)
            for i in range(KT):
                for k in range(KT):
                    mm(ps[:, i, :], wa[:, k, i * P:(i + 1) * P], w3[:, k, :], start=(k == 0), stop=False)
                mm(ps[:, i, i * P:(i + 1) * P], ident[:, :], ident3[:, :], start=False, stop=True).then_inc(c_ps, 1)

            def unit_lora(u, pieces):
                for k in pieces:
                    pe.wait_ge(usum, 3 * u + (4 if k == 2 else 3))
                    if k < 2:
                        for i in range(KT):
                            last = mm(ps[:, UBA + k, i * P:(i + 1) * P], s_au[:, k, i * P:(i + 1) * P],
                                      s_bu[:, k, col(u * P, P)], start=True, stop=True)
                    else:
                        last = mm(ps[:, UBA, :], s_ad[:, col(u * P, P)], s_bd, start=True, stop=True)
                    last.then_inc(uba_ps, 1)

            pe.wait_ge(c_ready, KT)
            pe.wait_ge(stacks_ready, 3)
            with pe.Fori(0, 2) as i:
                for t in range(8):
                    c, o = t // KT, t % KT
                    pe.wait_ge(x1_ready, 8 * i + t + 1)
                    for k in range(KT):
                        last = three(ps[:, t % 4, :], lambda h: cpair[:, h, k, o * P:(o + 1) * P],
                                     lambda h: xnT[:, h, k, bass.ds(i * (2 * CH) + c * CH, CH)], k == 0, k == KT - 1)
                    last.then_inc(x1_ps, 1)
                    if t == 0:
                        unit_lora(i, (0, 1))
                    if t == 5:
                        unit_lora(i, (2,))

            def gate_up(u, q, c):
                pe.wait_ge(uready, 3 * (u + 1))
                slot = slot_of(u)
                for g, (bank, done, read) in enumerate(((GATE, gate_ps, silu_done), (UP, up_ps, h_ready32))):
                    if not (isinstance(q, int) and q == 0):
                        pe.wait_ge(read, q)
                    for k in range(KT):
                        off = g * PC + k * P
                        last = three(ps[:, bank, :], lambda h: units[:, slot, h, off:off + P],
                                     lambda h: x1T[:, h, k, col(c * CH, CH)], k == 0, k == KT - 1)
                    last.then_inc(done, 1)

            def down(g, v, q, it, c):
                first, n = GROUPS[g]
                slot, r = slot_of(first + v), v % 2
                pe.wait_ge(h_ready, q + 1)
                for s in range(SPC):
                    if v == 0:
                        pe.wait_ge(down_read, SPC * it + s + 1)
                    add_x1 = v == n - 1 and g == len(GROUPS) - 1
                    last = three(ps[:, DOWN + s, :], lambda h: hffn[:, r, h, s * P:(s + 1) * P],
                                 lambda h: units[:, slot, h, 2 * PC:3 * PC], v == 0, v == n - 1 and not add_x1)
                    if add_x1:
                        for k in range(KT):
                            for h in range(2):
                                last = mm(ps[:, DOWN + s, k * P:(k + 1) * P], x1T[:, h, k, col(c * CH + s * P, P)],
                                          ident64[:, :], start=False, stop=(k == KT - 1 and h == 1))
                    if v == n - 1:
                        last.then_inc(down_ps, 1)

            def body(g, c, peeled):
                first, n = GROUPS[g]
                q = tiles_before[g] + c * n
                it = NCH * g + c
                new = GROUPS[g + 1][0] if g + 1 < len(GROUPS) else None
                for v in range(1, n + 1):
                    if v < n:
                        gate_up(first + v, q + v, c)
                    elif not peeled:
                        gate_up(first, q + n, c + 1)
                    elif new is not None:
                        gate_up(new, q + n, 0)
                    if new is not None:
                        if v == 1:
                            unit_lora(new + c, (0, 1))
                        if v == (3 if n > 2 else 2):
                            unit_lora(new + c, (2,))
                    down(g, v - 1, q + v - 1, it, c)

            pe.wait_ge(x1_ready, 4 + 16)
            gate_up(0, 0, 0)
            for g in range(len(GROUPS)):
                with pe.Fori(0, NCH - 1) as c:
                    body(g, c, False)
                body(g, NCH - 1, True)


def kernel(**inputs):
    import numpy as np
    import concourse.bacc as bacc
    from concourse.bass_utils import run_bass_kernel_spmd

    a = {n: np.asarray(v) for n, v in inputs.items()}
    ca, sa = a["L0_attn_codes_attn"], a["L0_attn_scales_attn"]
    cg, sg = a["L0_attn_codes_gu"], a["L0_attn_scales_gu"]
    cd, sd = a["L0_attn_codes_down"], a["L0_attn_scales_down"]
    ah, ad = a["L0_attn_lora_A_h"], a["L0_attn_lora_A_down"]
    ba, bg, bd = a["L0_attn_lora_B_attn"], a["L0_attn_lora_B_gu"], a["L0_attn_lora_B_down"]

    codes4 = np.stack([ca[0], ca[1], ca[2], ca[3].T]).reshape(4, KT, P, D).transpose(1, 0, 2, 3)
    scales3 = sa[0:3].reshape(3, KT, P, NB).transpose(2, 1, 0, 3).reshape(P, KT, 3 * NB)
    scales_o = sa[3].T.reshape(KT, 2, D)
    cgt = cg.transpose(0, 2, 1).reshape(2, KT, P, UNITS, P).transpose(3, 0, 2, 1, 4).reshape(UNITS, 2, P, PC)
    cdt = cd.T.reshape(UNITS, 1, P, D)
    ucodes = np.concatenate([cgt, cdt], 1)
    sgt = sg.transpose(0, 2, 1).reshape(2, KT, 2, UNITS, P).transpose(3, 0, 2, 1, 4).reshape(UNITS, 2, 2, PC)
    sdt = sd.T.reshape(UNITS, 1, 2, D)
    uscales = np.concatenate([sgt, sdt], 1)
    pos = np.arange(T) % S
    share = np.stack([np.where(pos >= VISION, 1.0 / ((S - VISION) * D), 0.0),
                      np.where(pos < VISION, 1.0 / (VISION * D), 0.0)], -1).astype(np.float32)

    arrays = {
        "x": a["L0_attn_x"].reshape(T, D),
        "attn_codes": codes4, "attn_scales": scales3, "attn_scales_o": scales_o,
        "unit_codes": ucodes, "unit_scales": uscales,
        "lora_bt": ba[0:3].transpose(0, 2, 1).reshape(3 * R, KT, P).transpose(1, 0, 2),
        "lora_a": ah[0:3].reshape(3 * R, D),
        "lora_a3": ah[3].reshape(R, KT, P).transpose(1, 0, 2),
        "lora_bt3": ba[3].T,
        "lora_au": ah[4:6].transpose(1, 0, 2).reshape(R, 2 * D),
        "lora_bu": bg.transpose(2, 0, 1).reshape(R, 2 * I),
        "lora_ad": ad, "lora_bd": bd.T,
        "gate_w": a["L0_ffn_gate_w"][0:D].reshape(KT, P, E).transpose(1, 0, 2),
        "gate_tail": a["L0_ffn_gate_w"][D:D + 1], "gate_b": a["L0_ffn_gate_b"].reshape(1, E),
        "w1": a["L0_ffn_w1"], "b1": a["L0_ffn_b1"].reshape(E, KT, P).transpose(0, 2, 1),
        "w2": a["L0_ffn_w2"], "b2": a["L0_ffn_b2"],
        "eye": np.eye(P, dtype=np.float32),
        "region": share.reshape(NST, P, 2).transpose(1, 0, 2),
    }
    arrays = {f"in_{n}": np.ascontiguousarray(v) for n, v in arrays.items()}
    nc = bacc.Bacc("TRN2", target_bir_lowering=False, num_devices=1)
    args = {n[3:]: nc.dram_tensor(n, v.shape, mybir.dt.from_np(v.dtype), kind="ExternalInput").ap()
            for n, v in arrays.items()}
    args["m_store"] = nc.dram_tensor("m_store", (B, NST // B, P, D), F32, kind="Internal").ap()
    args["out"] = nc.dram_tensor("out", (T, D), F32, kind="ExternalOutput").ap()
    build(nc, **args)
    r = run_bass_kernel_spmd(nc, [arrays], core_ids=[0])
    return r.results[0]["out"].reshape(B, S, D)
```

```python
from contextlib import ExitStack

import concourse.bass as bass
from concourse import mybir

F32 = mybir.dt.float32
F16 = mybir.dt.float16
I32 = mybir.dt.int32
ALU = mybir.AluOpType
ACT = mybir.ActivationFunctionType

NF4 = [-1.0, -0.6961928009986877, -0.5250730514526367, -0.39491748809814453, -0.28444138169288635,
       -0.18477343022823334, -0.09105003625154495, 0.0, 0.07958029955625534, 0.16093020141124725,
       0.24611230194568634, 0.33791524171829224, 0.44070982933044434, 0.5626170039176941,
       0.7229568362236023, 1.0]

P = 128
B, S, D = 2, 1024, 512
T = B * S
KT = D // P
NST = T // P
CH = 512
NCH = T // CH
SPC = CH // P
I = 1792
UNITS = I // P
R = 16
E = 3
NB = D // 64
PC = 512
WS = 64.0
AS, BS = 16.0, 4.0
EPS = 1e-5
VISION = int(S * 0.3)
GROUPS = [(0, 3), (3, 4), (7, 4), (11, 3)]
SLOTS = 8
ROT = 5


def slot_of(u):
    return (u + ROT) % SLOTS


def nf4_terms():
    v = NF4
    line = [(v[k + 1] - v[k], v[k] - (v[k + 1] - v[k]) * k) for k in range(1, 15, 2)]
    mid = 3
    rights = [(line[n + 1][0] - line[n][0], line[n + 1][1] - line[n][1]) for n in range(mid, 6)]
    lefts = [(line[n][0] - line[n - 1][0], line[n][1] - line[n - 1][1]) for n in range(mid, 0, -1)]
    steep = (v[1] - v[0]) - line[0][0]
    cap_at = 15.0 - ((v[15] - v[14]) - line[6][0]) / steep
    terms = [rights[0], (steep, -steep), lefts[0], rights[1], lefts[1], rights[2], lefts[2]]
    return line[mid][0] + steep, line[mid][1] - steep, steep * (cap_at - 1.0), terms


NF4_SLOPE, NF4_CONST, NF4_CAP, NF4_TERMS = nf4_terms()
NTERM = len(NF4_TERMS)
HR = 4
ADDS = 7
READ_BY = [1, 2, 2, 3, 4, 5, 6]
TERMS_NEEDED = [0, 1, 3, 4, 5, 6, 7, 7]
SUM_BEFORE = [0, 0, 0, 1, 2, 3, 4, 6]


def build(nc, x, attn_codes, attn_scales, attn_scales_o, unit_codes, unit_scales, lora_bt, lora_a,
          lora_a3, lora_bt3, lora_units, gate_w, gate_tail, gate_b, w1, b1, w2, b2,
          eye, region, m_store, out):
    ctx = ExitStack()
    with ctx:
        def sb(name, shape, dt):
            return ctx.enter_context(nc.sbuf_tensor(name, shape, dt))

        def sem(name):
            return ctx.enter_context(nc.semaphore(name))

        reg_a = sb("reg_a", [P, NST * D], F32)
        xnT = reg_a[:, :].bitcast(F16).rearrange("p (h k t) -> p h k t", h=2, k=KT)
        acc = reg_a[:, :].rearrange("p (s d) -> p s d", d=D)
        reg_b = sb("reg_b", [P, NST * D], F32)
        xs = reg_b[:, :].rearrange("p (s d) -> p s d", d=D)
        wpair = reg_b[:, 4096:8192].bitcast(F16).rearrange("p (w h k f) -> p w h k f", w=2, h=2, k=KT)
        wstage = reg_b[:, 0:4096].rearrange("p (w n) -> p w n", w=2)
        x1T = reg_b[:, :].bitcast(F16).rearrange("p (h k t) -> p h k t", h=2, k=KT)
        reg_c = sb("reg_c", [P, SLOTS * 3 * PC], F32)
        units = reg_c[:, :].bitcast(F16).rearrange("p (s h n) -> p s h n", s=SLOTS, h=2)
        mix = reg_c[:, 0:4096].rearrange("p (s d) -> p s d", d=D)
        NRAW = 2 * D + I + 2 * I + D
        raw = reg_c[:, 4096:4096 + NRAW]
        L0 = 4096 + NRAW
        la = reg_c[:, L0:L0 + D]
        lb = reg_c[:, L0 + D:L0 + D + P]
        b2p = reg_c[:, L0 + D + P:L0 + 2 * D + P].bitcast(F16).rearrange("p (s n) -> p s n", s=2)
        assert L0 + 2 * D + P <= SLOTS * 3 * PC
        reg_d = sb("reg_d", [P, 4096], F32)
        hmix = reg_d[:, :].bitcast(F16).rearrange("p (c h f t) -> p c h f t", c=2, h=2, f=KT)
        hffn = reg_d[:, 0:3 * CH].bitcast(F16).rearrange("p (r h t) -> p r h t", r=3, h=2)
        sgate = reg_d[:, 3 * CH:6 * CH].rearrange("p (r t) -> p r t", r=3)
        h32 = reg_d[:, 6 * CH:8 * CH].rearrange("p (r t) -> p r t", r=2)
        act32 = sb("act32", [P, 2, CH], F32)
        reg_e = sb("reg_e", [P, 2 * KT * D], F32)
        wa = reg_e[:, 0:KT * D].rearrange("p (k n) -> p k n", k=KT)
        w3 = reg_e[:, KT * D:2 * KT * D].rearrange("p (k n) -> p k n", k=KT)
        fin_g = reg_e[:, 0:SPC * D].rearrange("p (s d) -> p s d", s=SPC)
        fin_x = reg_e[:, SPC * D:2 * SPC * D].rearrange("p (s d) -> p s d", s=SPC)
        cpair = sb("cpair", [P, 2, KT, D], F16)
        stack = sb("stack", [P, NRAW], F16)
        s_au = stack[:, 0:2 * D].rearrange("p (g n) -> p g n", g=2)
        s_ad = stack[:, 2 * D:2 * D + I]
        s_bu = stack[:, 2 * D + I:2 * D + 3 * I].rearrange("p (g n) -> p g n", g=2)
        s_bd = stack[:, 2 * D + 3 * I:NRAW]
        STACK_PARTS = [(0, (2 * D + I) // 4, AS), (2 * D + I, (2 * I + D) // 4, BS)]
        codes = sb("codes", [P, 4, PC], I32)
        scl = sb("scl", [P, 3, PC], F32)
        term = sb("term", [P, HR, PC], F32)
        suma = sb("suma", [P, 3, PC], F32)
        sumb = sb("sumb", [P, PC], F32)
        tbias = sb("tbias", [P, 2, NTERM], F32)
        ascl = sb("ascl", [P, KT, 3 * NB], F32)
        b2r = scl[:, 1:3, :]
        ident = sb("ident", [P, P], F32)
        ident3 = sb("ident3", [P, P], F32)
        ident64 = sb("ident64", [P, P], F16)
        ones = sb("ones", [P, P], F32)
        ones16 = sb("ones16", [P, P], F16)
        share = sb("share", [P, NST, 2], F32)
        shared_abs = sb("shared_abs", [P, NST, 2], F32)
        abs_part = sb("abs_part", [P, B, 2], F32)
        bst = sb("bst", [P, NST, 6], F32)
        mv = sb("mv", [P, NST, 2], F32)
        std = sb("std", [P, NST], F32)
        rstd = sb("rstd", [P, NST], F32)
        epst = sb("epst", [P, 1], F32)
        absum = sb("absum", [P, NST], F32)
        gw = sb("gw", [P, KT, E], F32)
        gw6 = sb("gw6", [P, KT, 2 * E], F16)
        gtail = sb("gtail", [P, 2, E], F32)
        strength = sb("strength", [P, B, 2], F32)
        ratio = sb("ratio", [P, B], F32)
        addl = sb("addl", [P, B, E], F32)
        lgt = sb("lgt", [P, NST, E], F32)
        lgs = sb("lgs", [P, NST, E], F32)
        pr = sb("pr", [P, NST, E], F32)
        rt = sb("rt", [P, 8, NST], F32)
        coef = sb("coef", [P, B, 2, NST // B], F32)
        rk = sb("rk", [1, 12, B], F32)
        idx = sb("idx", [1, 8], I32)
        b1t = sb("b1t", [P, 2, KT], F32)

        ps = ctx.enter_context(nc.psum_tensor("ps", [P, 8, 512], F32))
        PRE, OUT, ABA, UBA, GATE, UP, DOWN = 0, 2, 4, 6, 0, 1, 2
        TBANKS, ROUTER = 6, 6
        STRENGTH = 128

        x_in = [sem(f"x_in{q}") for q in range(NCH)]
        eye_in = sem("eye_in")
        router_in = sem("router_in")
        attn_in = sem("attn_in")
        raw_zero = sem("raw_zero")
        raw_in = sem("raw_in")
        stack_hi = sem("stack_hi")
        stacks_ready = sem("stacks_ready")
        setup_done = sem("setup_done")
        ident_ready = sem("ident_ready")
        stats_step = sem("stats_step")
        stats_ready = sem("stats_ready")
        std_ready = sem("std_ready")
        rstd_ready = sem("rstd_ready")
        xn_ready = sem("xn_ready")
        abs_done = sem("abs_done")
        xt_ps = sem("xt_ps")
        xt_hi = sem("xt_hi")
        xt_lo = sem("xt_lo")
        gw_ready = sem("gw_ready")
        abs_ready = sem("abs_ready")
        router_ps = sem("router_ps")
        rt_step = sem("rt_step")
        lgs_ready = sem("lgs_ready")
        exp_ready = sem("exp_ready")
        idx_ready = sem("idx_ready")
        w_in = [sem(f"w{w + 1}_in") for w in range(2)]
        w_hi = [sem(f"w{w + 1}_hi") for w in range(2)]
        w_ready = [sem(f"w{w + 1}_ready") for w in range(2)]
        b1_in = [sem(f"b1_in{r}") for r in range(2)]
        b2_in = [sem(f"b2_in{r}") for r in range(2)]
        b2_hi = sem("b2_hi")
        b2_ready = sem("b2_ready")
        pre_ps = sem("pre_ps")
        act_ready = sem("act_ready")
        hmix_ready = sem("hmix_ready")
        out_ps = sem("out_ps")
        out0_read = sem("out0_read")
        out1_read = sem("out1_read")
        mix_stored = sem("mix_stored")
        mix_free = sem("mix_free")
        acodes_in = [sem(f"acodes_in{k}") for k in range(4)]
        ascl_in = sem("ascl_in")
        lb_in = sem("lb_in")
        aterm = sem("aterm")
        aread = sem("aread")
        ascaled = sem("ascaled")
        amerged = sem("amerged")
        aba_ps = sem("aba_ps")
        c_ps = sem("c_ps")
        c_hi = sem("c_hi")
        c_ready = sem("c_ready")
        x1_ps = sem("x1_ps")
        x1_hi = sem("x1_hi")
        x1_ready = sem("x1_ready")
        ucodes_in = [sem(f"ucodes_in{k}") for k in range(3)]
        uscl_in = [sem(f"uscl_in{k}") for k in range(3)]
        uterm = sem("uterm")
        uread = sem("uread")
        uscaled = sem("uscaled")
        usum = sem("usum")
        uhi = sem("uhi")
        uready = sem("uready")
        uba_ps = sem("uba_ps")
        gate_ps = sem("gate_ps")
        up_ps = sem("up_ps")
        silu_done = sem("silu_done")
        h_ready32 = sem("h_ready32")
        h_hi = sem("h_hi")
        h_ready = sem("h_ready")
        down_ps = sem("down_ps")
        down_read = sem("down_read")
        fm_in = [sem(f"fm_in{s}") for s in range(SPC)]
        fx_in = [sem(f"fx_in{s}") for s in range(SPC)]
        fgate = sem("fgate")
        fscaled = sem("fscaled")
        fbase = sem("fbase")
        fout = sem("fout")
        stored = [sem(f"stored{s}") for s in range(SPC)]

        block = ctx.enter_context(nc.Block())

        VEC_SEQ, SCA_SEQ = [], []
        for k in range(3):
            VEC_SEQ += [(k, 1), (k, 2)] + ([(k - 1, 10)] if k else []) + [(k, n) for n in range(3, 10)]
            SCA_SEQ += [(k, n) for n in range(4)] + ([(k - 1, 8)] if k else []) + [(k, n) for n in range(4, NTERM)]
        VEC_SEQ += [(2, 10)]
        SCA_SEQ += [(2, 8)]

        def part(seq, i, n):
            return seq[len(seq) * i // n:len(seq) * (i + 1) // n]

        VEC_CUTS, SCA_CUTS = [0, 6, 12, 18, 22], [0, 7, 11, 16, 20]

        tiles_before = [NCH * sum(n for _, n in GROUPS[:g]) for g in range(len(GROUPS))]

        def ring(v, n):
            return v % n % (3 if n % 2 else 2)

        def col(v, n):
            return slice(v, v + n) if isinstance(v, int) else bass.ds(v, n)

        @block.sync
        def _(sp):
            def load_x(q):
                sp.dma_start(xs[:, q * SPC:(q + 1) * SPC, :],
                             x[q * CH:(q + 1) * CH, :].rearrange("(s p) d -> p s d", p=P)).then_inc(x_in[q], 16)

            load_x(0)
            sp.dma_start(ident[:, :], eye).then_inc(eye_in, 16)
            load_x(1)
            for dst, src in ((gw[:, :, :], gate_w), (share[:, :, :], region), (gtail[:, 0, :], gate_tail.to_broadcast([P, E])),
                             (gtail[:, 1, :], gate_b.to_broadcast([P, E]))):
                sp.dma_start(dst, src).then_inc(router_in, 16)
            load_x(2)
            load_x(3)
            for dst, src in ((ascl[:, :, :], attn_scales), (la[0:3 * R, :], lora_a), (la[64:64 + R, :], lora_bt3)):
                sp.dma_start(dst, src).then_inc(attn_in, 16)
            sp.wait_ge(setup_done, 2)

            def load_attn(n):
                for k in range(4):
                    sp.wait_ge(amerged, 4 * n + k + 1)
                    sp.dma_start(codes[:, k, :],
                                 attn_codes[col(n, 1), k, :, :].rearrange("a p c -> p (a c)")).then_inc(acodes_in[k], 16)
                sp.dma_start(lb[0:3 * R, :], lora_bt[col(n, 1), :, :].rearrange("a r m -> r (a m)")).then_inc(lb_in, 16)
                sp.dma_start(lb[64:64 + R, :], lora_a3[col(n, 1), :, :].rearrange("a r m -> r (a m)")).then_inc(lb_in, 16)
                for half in range(2):
                    sp.dma_start(scl[64 * half:64 * half + 64, 0, :],
                                 attn_scales_o[col(n, 1), half, :].to_broadcast([64, PC])).then_inc(ascl_in, 16)

            def load_w(n, w, slot):
                j = sp.value_load(idx[0:1, col(n, 1)], min_val=0, max_val=E - 1)
                sp.wait_ge(w_ready[w], n + 1)
                if w == 0:
                    sp.dma_start(b1t[:, slot, :], b1[bass.ds(j, 1), :, :].rearrange("a p k -> p (a k)")).then_inc(b1_in[slot], 16)
                else:
                    for row in (0, 32):
                        sp.dma_start(b2r[row:row + 1, slot, :], b2[bass.ds(j, 1), :]).then_inc(b2_in[slot], 16)
                sp.dma_start(wstage[:, w, :].rearrange("p (k f) -> p k f", k=KT),
                             (w1, w2)[w][bass.ds(j, 1), :, :].rearrange("a (k p) f -> p (a k) f", p=P)).then_inc(w_in[w], 16)

            for b in range(B):
                sp.wait_ge(idx_ready, b + 1)
                for slot in range(2):
                    load_w(2 * b + slot, 0, slot)
                    load_w(2 * b + slot, 1, slot)
                    load_attn(2 * b + slot)
            load_w(2 * B, 0, 0)

            sp.wait_ge(amerged, 4 * 4 + 4)
            sp.wait_ge(b2_ready, 2 * B)
            with sp.Fori(0, UNITS) as u:
                for k in range(3):
                    sp.wait_ge(usum, 3 * u + k + 1)
                    sp.dma_start(codes[:, k, :],
                                 unit_codes[bass.ds(u, 1), k, :, :].rearrange("a p c -> p (a c)")).then_inc(ucodes_in[k], 16)
                    for half in range(2):
                        sp.dma_start(scl[64 * half:64 * half + 64, k, :],
                                     unit_scales[bass.ds(u, 1), k, half, :].to_broadcast([64, PC])).then_inc(uscl_in[k], 16)

            sp.wait_ge(c_ready, KT)
            sp.wait_ge(mix_stored, 16 * B)

            def load_fin(t, s):
                sp.dma_start(fin_g[:, s, :], m_store.rearrange("b s p d -> (b s) p d")[col(t, 1), :, :].rearrange("a p d -> p (a d)")).then_inc(fm_in[s], 16)
                sp.dma_start(fin_x[:, s, :], x.rearrange("(s p) d -> s p d", p=P)[col(t, 1), :, :].rearrange("a p d -> p (a d)")).then_inc(fx_in[s], 16)

            def store(c):
                for s in range(SPC):
                    t = SPC * c + s
                    sp.wait_ge(fout, t + 1)
                    sp.dma_start(out.rearrange("(s p) d -> s p d", p=P)[col(t, 1), :, :].rearrange("a p d -> p (a d)"), fin_x[:, s, :]).then_inc(stored[s], 16)

            for s in range(SPC):
                load_fin(s, s)
            with sp.Fori(0, NCH - 1) as c:
                store(c)
                for s in range(SPC):
                    sp.wait_ge(stored[s], 16 * c + 16)
                    load_fin(SPC * c + s + SPC, s)
            store(NCH - 1)
            for s in range(SPC):
                sp.wait_ge(stored[s], 16 * NCH)

        @block.gpsimd
        def _(gp):
            nc.gpsimd.memset(raw, 0.0).then_inc(raw_zero, 1)
            gp.wait_ge(raw_zero, 1)
            for q in range(4):
                gp.dma_start(raw[32 * q:32 * q + R, :], lora_units).then_inc(raw_in, 16)
            gp.sem_inc(mix_free, 1)
            with gp.Fori(0, B) as b:
                gp.wait_ge(out1_read, 8 * b + 16)
                gp.dma_start(m_store[bass.ds(b, 1), :, :, :].rearrange("a s p d -> p (a s) d"), mix).then_inc(mix_stored, 16)
                gp.wait_ge(mix_stored, 16 * b + 16)
                gp.sem_inc(mix_free, 1)

        @block.scalar
        def _(act):
            act.wait_ge(setup_done, 2)

            def stds(b):
                s0 = b * NST // B
                act.wait_ge(stats_ready, (b + 1) * NST // B)
                nc.scalar.activation(std[:, s0:s0 + NST // B], mv[:, s0:s0 + NST // B, 1], ACT.Sqrt,
                                     bias=epst[:, 0:1]).then_inc(std_ready, 1)

            def token_tiles(t0, t1):
                for t in range(t0, t1):
                    act.wait_ge(xn_ready, t + 1)
                    if t >= HR:
                        act.wait_ge(abs_done, t - HR + 1)
                    nc.scalar.activation(term[:, t % HR, :], xs[:, t, :], ACT.Abs, accum_out=absum[:, t:t + 1]).then_inc(abs_done, 1)
                    act.wait_ge(xt_ps, t + 1)
                    nc.scalar.activation(xnT[:, 0, :, t * P:(t + 1) * P],
                                         ps[:, t % TBANKS, :].rearrange("p (k t) -> p k t", k=KT), ACT.Copy).then_inc(xt_hi, 1)

            def exps(b):
                t0, t1 = b * NST // B, (b + 1) * NST // B
                act.wait_ge(lgs_ready, b + 1)
                nc.scalar.activation(pr[:, t0:t1, :], lgs[:, t0:t1, :], ACT.Exp).then_inc(exp_ready, 1)

            def nf4_term(e, codes_k, ws, done):
                nc.scalar.activation(term[:, e % HR, :], codes_k, ACT.Relu, bias=tbias[:, ws, e:e + 1],
                                     scale=NF4_TERMS[e][0] * (WS if ws else 1.0)).then_inc(done, 1)

            def term_free(e):
                if e >= HR:
                    return READ_BY[e - HR] + ADDS
                return READ_BY[e + HR if e + HR < NTERM else e]

            def attn_term(n, k, e):
                if e == 0:
                    act.wait_ge(acodes_in[k], 16 * n + 16)
                act.wait_ge(aread, ADDS * (4 * n + k) + term_free(e))
                nf4_term(e, codes[:, k, :], 0, aterm)

            def w_high(w):
                nc.scalar.activation(wpair[:, w, 0, :, :], wstage[:, w, :].rearrange("p (k f) -> p k f", k=KT),
                                     ACT.Copy, scale=WS).then_inc(w_hi[w], 1)

            def stack_high(n):
                for c0, width, scale in STACK_PARTS:
                    cols = col(c0 + n * width, width)
                    nc.scalar.activation(stack[:, cols], raw[:, cols], ACT.Copy, scale=scale).then_inc(stack_hi, 1)

            act.wait_ge(raw_in, 16 * 4)
            act.sem_inc(act_ready, 2)
            stds(0)
            token_tiles(0, 8)
            stds(1)
            exps(0)
            token_tiles(8, 12)
            act.wait_ge(abs_done, 12)
            act.wait_ge(w_in[0], 16)
            w_high(0)
            token_tiles(12, 16)
            exps(1)
            act.wait_ge(abs_done, NST)
            act.wait_ge(idx_ready, 2)
            with act.Fori(0, B) as b:
                for slot in range(2):
                    n = 2 * b + slot
                    j = act.value_load(idx[0:1, bass.ds(n, 1)], min_val=0, max_val=E - 1)
                    for expert, func in ((0, ACT.Tanh), (1, ACT.Gelu), (2, ACT.Silu)):
                        with act.If(j == expert):
                            act.wait_ge(b1_in[slot], 16 * b + 16)
                            for t in range(2 * KT):
                                c, f = t // KT, t % KT
                                act.wait_ge(pre_ps, 8 * n + t + 1)
                                act.wait_ge(hmix_ready, 8 * n + t + 1)
                                nc.scalar.activation(act32[:, t % 2, :], ps[:, PRE + t % 2, :], func,
                                                     bias=b1t[:, slot, f:f + 1], scale=1.0 / WS)
                                nc.scalar.activation(hmix[:, c, 0, f, :], ps[:, PRE + t % 2, :], func,
                                                     bias=b1t[:, slot, f:f + 1], scale=1.0 / WS).then_inc(act_ready, 1)
                                if t == 0:
                                    act.wait_ge(w_in[1], 16 * n + 16)
                                    w_high(1)
                                if t == 5:
                                    stack_high(n)
                                for e in part(range(NTERM), t % 4, 4):
                                    attn_term(n, t // 4, e)
                    act.wait_ge(w_in[0], 16 * n + 32)
                    w_high(0)
                    for s in range(8):
                        if slot == 0:
                            if s == 0:
                                act.wait_ge(mix_free, b + 1)
                            act.wait_ge(out_ps, 8 * n + s + 1)
                            nc.scalar.activation(mix[:, s, :], ps[:, OUT + s % 2, :], ACT.Copy,
                                                 scale=coef[:, bass.ds(b, 1), 0, s]).then_inc(out0_read, 1)
                        for e in part(range(NTERM), s % 4, 4):
                            attn_term(n, 2 + s // 4, e)

            def unit_step(u, slot, k, e):
                p = 3 * u + k
                if e == 8:
                    act.wait_ge(usum, p + 4)
                    nc.scalar.activation(units[:, col(slot, 1), 0, k * PC:(k + 1) * PC].rearrange("p a n -> p (a n)"),
                                         suma[:, k, :], ACT.Copy).then_inc(uhi, 1)
                    return
                if e == 0:
                    act.wait_ge(ucodes_in[k], 16 * u + 16)
                act.wait_ge(uread, ADDS * p + term_free(e))
                nf4_term(e, codes[:, k, :], 1, uterm)

            for k in range(KT):
                for piece, e in SCA_SEQ[SCA_CUTS[k]:SCA_CUTS[k + 1]]:
                    unit_step(0, slot_of(0), piece, e)
                act.wait_ge(c_ps, k + 1)
                nc.scalar.activation(cpair[:, 0, k, :], ps[:, k, :], ACT.Copy, scale=WS / 3.0).then_inc(c_hi, 1)
            for piece, e in SCA_SEQ[SCA_CUTS[KT]:]:
                unit_step(0, slot_of(0), piece, e)

            with act.Fori(0, 2) as i:
                for t in range(8):
                    c, o = t // KT, t % KT
                    act.wait_ge(x1_ps, 8 * i + t + 1)
                    nc.scalar.activation(x1T[:, 0, o, bass.ds(i * (2 * CH) + c * CH, CH)], ps[:, t % 4, :], ACT.Copy,
                                         scale=1.0 / WS).then_inc(x1_hi, 1)
                    for k, e in part(SCA_SEQ, t, 8):
                        unit_step(i + 1, i + slot_of(1), k, e)

            def silu(q, r):
                act.wait_ge(gate_ps, q + 1)
                nc.scalar.activation(sgate[:, r, :], ps[:, GATE, :], ACT.Silu, scale=1.0 / WS).then_inc(silu_done, 1)

            def high(q, r):
                act.wait_ge(h_ready32, q + 1)
                nc.scalar.activation(hffn[:, r, 0, :], h32[:, r % 2, :], ACT.Copy).then_inc(h_hi, 1)

            def body(g, c, last):
                first, n = GROUPS[g]
                q = tiles_before[g] + c * n
                it = NCH * g + c
                new, width = GROUPS[g + 1] if g + 1 < len(GROUPS) else (None, 0)
                for v in range(1, n + 1):
                    steps = part(SCA_SEQ, v - 1, n) if new is not None and not (isinstance(c, int) and c >= width) else []
                    if not (last and v == n):
                        silu(q + v, ring(v, n))
                    for k, e in steps[:2]:
                        unit_step(new + c, slot_of(new) + c, k, e)
                    if not (last and v == n):
                        high(q + v, ring(v, n))
                    for k, e in steps[2:]:
                        unit_step(new + c, slot_of(new) + c, k, e)
                    if new is None and v > 1:
                        for s in part(range(SPC), v - 2, n - 1):
                            act.wait_ge(fm_in[s], 16 * c + 16)
                            nc.scalar.activation(fin_g[:, s, :], fin_g[:, s, :], ACT.Silu).then_inc(fgate, 1)
                if g == 0:
                    for s in range(SPC):
                        act.wait_ge(down_ps, SPC * it + s + 1)
                        nc.scalar.activation(acc[:, col(SPC * c + s, 1), :].rearrange("p a d -> p (a d)"), ps[:, DOWN + s, :],
                                             ACT.Copy).then_inc(down_read, 1)

            act.wait_ge(mix_free, B + 1)
            silu(0, 0)
            high(0, 0)
            for g in range(len(GROUPS)):
                with act.Fori(0, NCH - 1) as c:
                    body(g, c, False)
                body(g, NCH - 1, g == len(GROUPS) - 1)

        @block.vector
        def _(vec):
            vector = nc.vector
            for e, (_, bias) in enumerate(NF4_TERMS):
                vector.memset(tbias[:, 0, e:e + 1], bias)
                vector.memset(tbias[:, 1, e:e + 1], bias * WS)
            vector.memset(epst[:, :], EPS)
            vector.memset(ones[:, :], 1.0)
            vector.memset(ones16[:, :], 1.0).then_inc(setup_done, 1)
            vector.memset(idx[:, :], 0)
            vector.memset(b2r, 0.0).then_inc(setup_done, 1)
            vec.sem_inc(hmix_ready, 2)
            vec.sem_inc(out1_read, 8)
            vec.sem_inc(aread, ADDS)
            vec.sem_inc(amerged, 4)
            vec.sem_inc(uread, ADDS)
            vec.sem_inc(usum, 3)
            vec.sem_inc(x1_ready, 4)
            vec.sem_inc(down_read, 4)
            for w in range(2):
                vec.sem_inc(w_ready[w], 1)

            def stats(b):
                for q in range(b * NCH // B, (b + 1) * NCH // B):
                    vec.wait_ge(x_in[q], 16)
                    for t in range(q * SPC, (q + 1) * SPC):
                        vector.bn_stats(bst[:, t, :], xs[:, t, :]).then_inc(stats_step, 1)
                    for t in range(q * SPC, (q + 1) * SPC):
                        vec.wait_ge(stats_step, t + 1)
                        vector.bn_aggr(mv[:, t, :], bst[:, t, :]).then_inc(stats_ready, 1)

            def normalise(b):
                vec.wait_ge(std_ready, b + 1)
                t0, t1 = b * NST // B, (b + 1) * NST // B
                vector.reciprocal(rstd[:, t0:t1], std[:, t0:t1]).then_inc(rstd_ready, 1)
                vec.wait_ge(rstd_ready, b + 1)
                for t in range(t0, t1):
                    vector.tensor_scalar(xs[:, t, :], xs[:, t, :], mv[:, t, 0:1], rstd[:, t:t + 1], ALU.subtract,
                                         ALU.mult).then_inc(xn_ready, 1)

            def token_low(t0, t1):
                for t in range(t0, t1):
                    vec.wait_ge(xt_hi, t + 1)
                    vector.tensor_tensor(xnT[:, 1, :, t * P:(t + 1) * P], ps[:, t % TBANKS, :].rearrange("p (k t) -> p k t", k=KT),
                                         xnT[:, 0, :, t * P:(t + 1) * P], ALU.subtract).then_inc(xt_lo, 1)

            linked = [0]

            def link(ins):
                linked[0] += 1
                ins.then_inc(rt_step, 1)
                vec.wait_ge(rt_step, linked[0])

            def abs_sums(b):
                t0, t1 = b * NST // B, (b + 1) * NST // B
                vec.wait_ge(abs_done, t1)
                link(vector.tensor_tensor(shared_abs[:, t0:t1, :], share[:, t0:t1, :],
                                          absum[:, t0:t1].unsqueeze(2).to_broadcast([P, NST // B, 2]), ALU.mult))
                vector.tensor_reduce(abs_part[:, b, :], shared_abs[:, t0:t1, :].rearrange("p s r -> p r s"),
                                     mybir.AxisListType.X, ALU.add).then_inc(abs_ready, 1)

            def router(b):
                t0, t1 = b * NST // B, (b + 1) * NST // B
                n = NST // B
                lg, ls, prb, r = lgt[:, t0:t1, :], lgs[:, t0:t1, :], pr[:, t0:t1, :], rt[:, :, t0:t1]
                vec.wait_ge(router_ps, b + 1)
                raw_logits = ps[:, ROUTER + b, 0:2 * E * n].rearrange("p (t e) -> p t e", e=2 * E)
                vector.tensor_copy(ls, raw_logits[:, :, E:2 * E])
                link(vector.tensor_copy(strength[:, b, :], ps[:, ROUTER + b, STRENGTH:STRENGTH + 2]))
                vector.tensor_tensor(lg, raw_logits[:, :, 0:E], ls, ALU.add)
                link(vector.tensor_scalar(ratio[:, b:b + 1], strength[:, b, 1:2], 1e-8, None, ALU.add))
                link(vector.reciprocal(ratio[:, b:b + 1], ratio[:, b:b + 1]))
                link(vector.tensor_tensor(ratio[:, b:b + 1], ratio[:, b:b + 1], strength[:, b, 0:1], ALU.mult))
                link(vector.scalar_tensor_tensor(addl[:, b, :], gtail[:, 0, :], ratio[:, b:b + 1], gtail[:, 1, :], ALU.mult, ALU.add))
                link(vector.scalar_tensor_tensor(lg, lg, 1.0 / WS, addl[:, b:b + 1, :].to_broadcast([P, n, E]), ALU.mult, ALU.add))
                link(vector.tensor_tensor(r[:, 0, :], lg[:, :, 0], lg[:, :, 1], ALU.max))
                link(vector.tensor_tensor(r[:, 0, :], r[:, 0, :], lg[:, :, 2], ALU.max))
                vector.tensor_tensor(ls, lg, r[:, 0, :].unsqueeze(2).to_broadcast([P, n, E]), ALU.subtract).then_inc(lgs_ready, 1)
                vec.wait_ge(exp_ready, b + 1)
                link(vector.tensor_tensor(r[:, 1, :], prb[:, :, 0], prb[:, :, 1], ALU.add))
                link(vector.tensor_tensor(r[:, 1, :], r[:, 1, :], prb[:, :, 2], ALU.add))
                link(vector.reciprocal(r[:, 1, :], r[:, 1, :]))
                link(vector.tensor_tensor(prb, prb, r[:, 1, :].unsqueeze(2).to_broadcast([P, n, E]), ALU.mult))
                p0t = [pr[0:1, t0, e:e + 1] for e in range(E)]
                k = rk[:, :, b:b + 1]
                for row, a, b_, op in ((0, 1, 0, ALU.is_gt), (1, 2, 0, ALU.is_gt), (2, 0, 1, ALU.is_ge),
                                       (3, 2, 1, ALU.is_gt), (4, 0, 2, ALU.is_ge), (5, 1, 2, ALU.is_ge)):
                    last = vector.tensor_tensor(k[:, row, :], p0t[a], p0t[b_], op)
                link(last)
                for e in (1, 2):
                    last = vector.tensor_tensor(k[:, 6 + e, :], k[:, 2 * e, :], k[:, 2 * e + 1, :], ALU.add)
                link(last)
                for choice in range(2):
                    vector.tensor_scalar(k[:, 9, :], k[:, 7, :], float(choice), None, ALU.is_equal)
                    link(vector.tensor_scalar(k[:, 10, :], k[:, 8, :], float(choice), 2.0, ALU.is_equal, ALU.mult))
                    link(vector.tensor_tensor(k[:, 11, :], k[:, 9, :], k[:, 10, :], ALU.add))
                    last = vector.tensor_scalar(idx[:, 2 * b + choice:2 * b + choice + 1], k[:, 11, :], float(E - 1), None, ALU.min)
                last.then_inc(idx_ready, 1)
                vector.tensor_tensor(r[:, 2, :], prb[:, :, 0], prb[:, :, 1], ALU.max)
                link(vector.tensor_tensor(r[:, 3, :], prb[:, :, 0], prb[:, :, 1], ALU.min))
                vector.tensor_tensor(r[:, 4, :], r[:, 2, :], prb[:, :, 2], ALU.max)
                link(vector.tensor_tensor(r[:, 5, :], r[:, 2, :], prb[:, :, 2], ALU.min))
                link(vector.tensor_tensor(r[:, 5, :], r[:, 5, :], r[:, 3, :], ALU.max))
                link(vector.tensor_tensor(r[:, 6, :], r[:, 4, :], r[:, 5, :], ALU.add))
                link(vector.tensor_scalar(r[:, 6, :], r[:, 6, :], 1e-8, None, ALU.add))
                link(vector.reciprocal(r[:, 6, :], r[:, 6, :]))
                for choice in range(2):
                    link(vector.scalar_tensor_tensor(coef[:, b, choice, :], r[:, 4 + choice, :], 1.0 / WS, r[:, 6, :], ALU.mult, ALU.mult))

            def addition(k, step, codes_k, ws, done):
                a, b_ = suma[:, k, :], sumb[:, :]
                if step == 1:
                    ins = vector.scalar_tensor_tensor(a, codes_k, NF4_SLOPE * (WS if ws else 1.0), term[:, 0, :],
                                                      ALU.mult, ALU.add)
                elif step == 2:
                    ins = vector.scalar_tensor_tensor(b_, term[:, 1, :], NF4_CAP * (WS if ws else 1.0), term[:, 2, :],
                                                      ALU.min, ALU.add)
                elif step < 7:
                    s = a if step % 2 else b_
                    ins = vector.tensor_tensor(s, s, term[:, step % HR, :], ALU.add)
                else:
                    ins = vector.tensor_tensor(a, a, b_, ALU.subtract)
                ins.then_inc(done, 1)

            def attn_step(n, k, step):
                p = 4 * n + k
                if step <= ADDS:
                    vec.wait_ge(aterm, NTERM * p + TERMS_NEEDED[step])
                    if step > 2:
                        vec.wait_ge(aread, ADDS * p + ADDS + SUM_BEFORE[step])
                    addition(k % 3, step, codes[:, k, :], 0, aread)
                    return
                blocks = "p (b c) -> p b c"
                target = (wa if k < 3 else w3)[:, col(n, 1), :].rearrange("p a d -> p (a d)")
                mine = suma[:, k % 3, :]
                if step == 8:
                    vec.wait_ge(aread, ADDS * p + 2 * ADDS)
                    dst = target if k in (0, 3) else mine
                    if k == 3:
                        vec.wait_ge(ascl_in, 32 * n + 32)
                        vector.scalar_tensor_tensor(dst, mine, NF4_CONST, scl[:, 0, :], ALU.add, ALU.mult).then_inc(ascaled, 1)
                    else:
                        scales = ascl[:, col(n, 1), k * NB:(k + 1) * NB].rearrange("p a b -> p (a b)")
                        vector.scalar_tensor_tensor(dst.rearrange(blocks, b=NB), mine.rearrange(blocks, b=NB), NF4_CONST,
                                                    scales.unsqueeze(2).to_broadcast([P, NB, D // NB]), ALU.add,
                                                    ALU.mult).then_inc(ascaled, 1)
                else:
                    vec.wait_ge(ascaled, p + 1)
                    vec.wait_ge(amerged, p + 4)
                    if k in (0, 3):
                        vec.wait_ge(aba_ps, 2 * n + (1 if k == 0 else 2))
                        other = ps[:, ABA + (k == 3), :]
                    else:
                        other = mine
                    vector.tensor_tensor(target, other, target, ALU.add).then_inc(amerged, 1)

            ATTN_EVENT = [[(-1, 8), (0, 1)], [(-1, 9), (0, 2)], [(0, 3), (0, 4)], [(0, 5), (0, 6), (0, 7)]]

            def w_low(n, w):
                vec.wait_ge(w_hi[w], n + 1)
                vector.scalar_tensor_tensor(wpair[:, w, 1, :, :].rearrange("p k f -> p (k f)"), wstage[:, w, :], WS,
                                            wpair[:, w, 0, :, :].rearrange("p k f -> p (k f)"), ALU.mult,
                                            ALU.subtract).then_inc(w_ready[w], 1)

            def stack_low(n):
                (a0, aw, ascale), (b0, bw, bscale) = STACK_PARTS
                vec.wait_ge(stack_hi, 2 * n + 2)
                for p0, rows, cols, scale in ((64, 64, col(a0 + n * aw, aw), ascale), (32, 32, col(b0 + n * bw, bw), bscale),
                                              (96, 32, col(b0 + n * bw, bw), bscale)):
                    vector.scalar_tensor_tensor(stack[p0:p0 + rows, cols], raw[p0:p0 + rows, cols], scale,
                                                stack[p0:p0 + rows, cols], ALU.mult, ALU.subtract).then_inc(stacks_ready, 1)

            stats(0)
            normalise(0)
            stats(1)
            vec.wait_ge(eye_in, 16)
            vector.tensor_scalar(ident3[:, :], ident[:, :], 3.0, None, ALU.mult)
            vector.tensor_scalar(ident64[:, :], ident[:, :], WS, None, ALU.mult).then_inc(ident_ready, 1)
            vec.wait_ge(router_in, 16 * 4)
            vector.tensor_scalar(gw6[:, :, 0:E], gw[:, :, :], WS, None, ALU.mult).then_inc(gw_ready, 1)
            vec.wait_ge(gw_ready, 1)
            vector.scalar_tensor_tensor(gw6[:, :, E:2 * E], gw[:, :, :], WS, gw6[:, :, 0:E], ALU.mult,
                                        ALU.subtract).then_inc(gw_ready, 1)
            token_low(0, 8)
            abs_sums(0)
            normalise(1)
            router(0)
            token_low(8, 12)
            w_low(0, 0)
            token_low(12, 16)
            abs_sums(1)
            router(1)
            vec.wait_ge(attn_in, 16 * 3)
            with vec.Fori(0, B) as b:
                for slot in range(2):
                    n = 2 * b + slot
                    for t in range(2 * KT):
                        c, f = t // KT, t % KT
                        vec.wait_ge(act_ready, 8 * n + t + 3)
                        vector.tensor_tensor(hmix[:, c, 1, f, :], act32[:, t % 2, :], hmix[:, c, 0, f, :],
                                             ALU.subtract).then_inc(hmix_ready, 1)
                        if t == 0:
                            w_low(n, 1)
                            vec.wait_ge(b2_in[slot], 32 * b + 32)
                            vector.tensor_scalar(b2p[0:33, slot, :], b2r[0:33, slot, :], WS, None, ALU.mult).then_inc(b2_hi, 1)
                            vec.wait_ge(b2_hi, n + 1)
                            vector.scalar_tensor_tensor(b2p[32:33, slot, :], b2r[32:33, slot, :], WS, b2p[32:33, slot, :],
                                                        ALU.mult, ALU.subtract).then_inc(b2_ready, 1)
                        if t == 6:
                            stack_low(n)
                        for dk, step in ATTN_EVENT[t % 4]:
                            if t // 4 + dk >= 0:
                                attn_step(n, t // 4 + dk, step)
                    w_low(n + 1, 0)
                    for s in range(8):
                        if slot == 1:
                            vec.wait_ge(out_ps, 8 * n + s + 1)
                            if s == 0:
                                vec.wait_ge(out0_read, 8 * b + 8)
                            vector.scalar_tensor_tensor(mix[:, s, :], ps[:, OUT + s % 2, :], coef[:, bass.ds(b, 1), 1, s],
                                                        mix[:, s, :], ALU.mult, ALU.add).then_inc(out1_read, 1)
                        for dk, step in ATTN_EVENT[s % 4]:
                            attn_step(n, 2 + s // 4 + dk, step)
                    attn_step(n, 3, 8)
                    attn_step(n, 3, 9)

            def unit_step(u, slot, k, step):
                p = 3 * u + k
                if step <= ADDS:
                    vec.wait_ge(uterm, NTERM * p + TERMS_NEEDED[step])
                    if step > 2:
                        vec.wait_ge(uread, ADDS * p + ADDS + SUM_BEFORE[step])
                    addition(k, step, codes[:, k, :], 1, uread)
                elif step == 8:
                    vec.wait_ge(uread, ADDS * p + 2 * ADDS)
                    vec.wait_ge(uscl_in[k], 32 * u + 32)
                    vector.scalar_tensor_tensor(suma[:, k, :], suma[:, k, :], NF4_CONST * WS, scl[:, k, :], ALU.add,
                                                ALU.mult).then_inc(uscaled, 1)
                elif step == 9:
                    vec.wait_ge(uscaled, p + 1)
                    vec.wait_ge(uba_ps, p + 1)
                    vector.tensor_tensor(suma[:, k, :], ps[:, UBA + k % 2, :], suma[:, k, :], ALU.add).then_inc(usum, 1)
                else:
                    vec.wait_ge(uhi, p + 1)
                    high = units[:, col(slot, 1), 0, k * PC:(k + 1) * PC].rearrange("p a n -> p (a n)")
                    low = units[:, col(slot, 1), 1, k * PC:(k + 1) * PC].rearrange("p a n -> p (a n)")
                    vector.tensor_tensor(low, suma[:, k, :], high, ALU.subtract).then_inc(uready, 1)

            for k in range(KT):
                for piece, step in VEC_SEQ[VEC_CUTS[k]:VEC_CUTS[k + 1]]:
                    unit_step(0, slot_of(0), piece, step)
                vec.wait_ge(c_hi, k + 1)
                vector.scalar_tensor_tensor(cpair[:, 1, k, :], ps[:, k, :], WS / 3.0, cpair[:, 0, k, :], ALU.mult,
                                            ALU.subtract).then_inc(c_ready, 1)
            for piece, step in VEC_SEQ[VEC_CUTS[KT]:]:
                unit_step(0, slot_of(0), piece, step)

            with vec.Fori(0, 2) as i:
                for t in range(8):
                    c, o = t // KT, t % KT
                    vec.wait_ge(x1_hi, 8 * i + t + 1)
                    cols = bass.ds(i * (2 * CH) + c * CH, CH)
                    vector.scalar_tensor_tensor(x1T[:, 1, o, cols], ps[:, t % 4, :], 1.0 / WS, x1T[:, 0, o, cols],
                                                ALU.mult, ALU.subtract).then_inc(x1_ready, 1)
                    for k, step in part(VEC_SEQ, t, 8):
                        unit_step(i + 1, i + slot_of(1), k, step)

            def hidden(q, r):
                vec.wait_ge(up_ps, q + 1)
                vec.wait_ge(silu_done, q + 1)
                vector.scalar_tensor_tensor(h32[:, r % 2, :], ps[:, UP, :], 1.0 / WS, sgate[:, r, :], ALU.mult,
                                            ALU.mult).then_inc(h_ready32, 1)

            def low(q, r):
                vec.wait_ge(h_hi, q + 1)
                vector.tensor_tensor(hffn[:, r, 1, :], h32[:, r % 2, :], hffn[:, r, 0, :], ALU.subtract).then_inc(h_ready, 1)

            def base(c, s):
                t = SPC * c + s
                mine = acc[:, col(t, 1), :].rearrange("p a d -> p (a d)")
                vec.wait_ge(fgate, t + 1)
                vector.scalar_tensor_tensor(mine, mine, 1.0 / WS, fin_g[:, s, :], ALU.mult, ALU.mult).then_inc(fscaled, 1)
                vec.wait_ge(fscaled, t + 1)
                vec.wait_ge(fx_in[s], 16 * c + 16)
                vector.tensor_tensor(fin_x[:, s, :], mine, fin_x[:, s, :], ALU.add).then_inc(fbase, 1)

            def output(c, it, s):
                t = SPC * c + s
                vec.wait_ge(down_read, SPC * it + s + 5)
                vec.wait_ge(fbase, t + 1)
                vector.tensor_tensor(fin_x[:, s, :], fin_g[:, s, :], fin_x[:, s, :], ALU.add).then_inc(fout, 1)

            def body(g, c, last):
                first, n = GROUPS[g]
                q = tiles_before[g] + c * n
                it = NCH * g + c
                new, width = GROUPS[g + 1] if g + 1 < len(GROUPS) else (None, 0)
                for v in range(1, n + 1):
                    steps = part(VEC_SEQ, v - 1, n) if new is not None and not (isinstance(c, int) and c >= width) else []
                    if not (last and v == n):
                        hidden(q + v, ring(v, n))
                    for k, step in steps[:2]:
                        unit_step(new + c, slot_of(new) + c, k, step)
                    if not (last and v == n):
                        low(q + v, ring(v, n))
                    for k, step in steps[2:]:
                        unit_step(new + c, slot_of(new) + c, k, step)
                    if new is None and v > 1:
                        for s in part(range(SPC), v - 2, n - 1):
                            base(c, s)
                if 0 < g < len(GROUPS) - 1:
                    for s in range(SPC):
                        vec.wait_ge(down_ps, SPC * it + s + 1)
                        mine = acc[:, col(SPC * c + s, 1), :].rearrange("p a d -> p (a d)")
                        vector.tensor_tensor(mine, ps[:, DOWN + s, :], mine, ALU.add).then_inc(down_read, 1)
                if new is None:
                    for s in range(SPC):
                        vec.wait_ge(down_ps, SPC * it + s + 1)
                        vector.scalar_tensor_tensor(fin_g[:, s, :], ps[:, DOWN + s, :], 1.0 / WS, fin_g[:, s, :], ALU.mult,
                                                    ALU.mult).then_inc(down_read, 1)
                        if s:
                            output(c, it, s - 1)
                    output(c, it, SPC - 1)

            hidden(0, 0)
            low(0, 0)
            for g in range(len(GROUPS)):
                if g == 1:
                    vec.wait_ge(down_read, 4 + SPC * NCH)
                with vec.Fori(0, NCH - 1) as c:
                    body(g, c, False)
                body(g, NCH - 1, g == len(GROUPS) - 1)

        @block.tensor
        def _(pe):
            mm = nc.tensor.matmul

            def three(dst, stationary, moving, first, last):
                mm(dst, stationary(0), moving(0), start=first, stop=False)
                mm(dst, stationary(0), moving(1), start=False, stop=False)
                return mm(dst, stationary(1), moving(0), start=False, stop=last)

            pe.wait_ge(eye_in, 16)

            def transposes(b):
                for t in range(b * NST // B, (b + 1) * NST // B):
                    pe.wait_ge(xn_ready, t + 1)
                    if t >= TBANKS:
                        pe.wait_ge(xt_lo, t - TBANKS + 1)
                    for k in range(KT):
                        last = nc.tensor.transpose(ps[:, t % TBANKS, k * P:(k + 1) * P], xs[:, t, k * P:(k + 1) * P], ident[:, :])
                    last.then_inc(xt_ps, 1)

            def router(b):
                for t in range(b * NST // B, (b + 1) * NST // B):
                    pe.wait_ge(xt_lo, t + 1)
                    c0 = 2 * E * (t - b * NST // B)
                    for k in range(KT):
                        for h in range(2):
                            mm(ps[:, ROUTER + b, c0:c0 + 2 * E], xnT[:, h, k, t * P:(t + 1) * P], gw6[:, k, :],
                               start=(k == 0 and h == 0), stop=(k == KT - 1 and h == 1))
                pe.wait_ge(abs_ready, b + 1)
                mm(ps[:, ROUTER + b, STRENGTH:STRENGTH + 2], ones[:, :], abs_part[:, b, :], start=True,
                   stop=True).then_inc(router_ps, 1)

            transposes(0)
            pe.wait_ge(gw_ready, 2)
            router(0)
            transposes(1)
            router(1)
            pe.wait_ge(attn_in, 16 * 3)

            with pe.Fori(0, B) as b:
                for slot in range(2):
                    n = 2 * b + slot
                    pe.wait_ge(w_ready[0], n + 2)
                    for t in range(2 * KT):
                        c, f = t // KT, t % KT
                        pe.wait_ge(act_ready, 8 * n + t + 1)
                        for k in range(KT):
                            last = three(ps[:, PRE + t % 2, :], lambda h: wpair[:, 0, h, k, f * P:(f + 1) * P],
                                         lambda h: xnT[:, h, k, bass.ds(b * S + c * CH, CH)], k == 0, k == KT - 1)
                        last.then_inc(pre_ps, 1)
                        if t == 2:
                            pe.wait_ge(lb_in, 32 * n + 32)
                            pe.wait_ge(amerged, 4 * n + 4)
                            mm(ps[:, ABA, :], lb[0:3 * R, :], la[0:3 * R, :], start=True, stop=True).then_inc(aba_ps, 1)
                            mm(ps[:, ABA + 1, :], lb[64:64 + R, :], la[64:64 + R, :], start=True, stop=True).then_inc(aba_ps, 1)
                    pe.wait_ge(w_ready[1], n + 2)
                    pe.wait_ge(b2_ready, n + 1)
                    for s in range(8):
                        c = s // SPC
                        if slot == 0:
                            if s < 2:
                                pe.wait_ge(out1_read, 8 * b + 7 + s)
                            else:
                                pe.wait_ge(out0_read, 8 * b + s - 1)
                        elif s < 2:
                            pe.wait_ge(out0_read, 8 * b + 7 + s)
                        else:
                            pe.wait_ge(out1_read, 8 * b + 7 + s)
                        pe.wait_ge(hmix_ready, 8 * n + 4 * c + 6)
                        mm(ps[:, OUT + s % 2, :], ones16[0:33, :], b2p[0:33, slot, :], start=True, stop=False)
                        tok = slice((s % SPC) * P, (s % SPC + 1) * P)
                        for f in range(KT):
                            last = three(ps[:, OUT + s % 2, :], lambda h: hmix[:, c, h, f, tok],
                                         lambda h: wpair[:, 1, h, f, :], False, f == KT - 1)
                        last.then_inc(out_ps, 1)

            def unit_lora(u, pieces):
                for k in pieces:
                    pe.wait_ge(usum, 3 * u + (4 if k == 2 else 3))
                    if k < 2:
                        for i in range(KT):
                            last = mm(ps[:, UBA + k, i * P:(i + 1) * P], s_au[:, k, i * P:(i + 1) * P],
                                      s_bu[:, k, col(u * P, P)], start=True, stop=True)
                    else:
                        last = mm(ps[:, UBA, :], s_ad[:, col(u * P, P)], s_bd, start=True, stop=True)
                    last.then_inc(uba_ps, 1)

            pe.wait_ge(ident_ready, 1)
            pe.wait_ge(amerged, 4 * 4 + 4)
            pe.wait_ge(act_ready, 8 * 4 + 2)
            pe.wait_ge(out1_read, 8 * B + 8)
            pe.wait_ge(stacks_ready, 3 * 4)
            unit_lora(0, (0, 1))
            for i in range(KT):
                if i == 2:
                    unit_lora(0, (2,))
                for k in range(KT):
                    mm(ps[:, i, :], wa[:, k, i * P:(i + 1) * P], w3[:, k, :], start=(k == 0), stop=False)
                mm(ps[:, i, i * P:(i + 1) * P], ident[:, :], ident3[:, :], start=False, stop=True).then_inc(c_ps, 1)

            pe.wait_ge(c_ready, KT)
            with pe.Fori(0, 2) as i:
                for t in range(8):
                    c, o = t // KT, t % KT
                    pe.wait_ge(x1_ready, 8 * i + t + 1)
                    for k in range(KT):
                        last = three(ps[:, t % 4, :], lambda h: cpair[:, h, k, o * P:(o + 1) * P],
                                     lambda h: xnT[:, h, k, bass.ds(i * (2 * CH) + c * CH, CH)], k == 0, k == KT - 1)
                    last.then_inc(x1_ps, 1)
                    if t == 0:
                        unit_lora(i + 1, (0, 1))
                    if t == 5:
                        unit_lora(i + 1, (2,))

            def gate_up(u, q, c):
                pe.wait_ge(uready, 3 * (u + 1))
                slot = slot_of(u)
                for g, (bank, done, read) in enumerate(((GATE, gate_ps, silu_done), (UP, up_ps, h_ready32))):
                    if not (isinstance(q, int) and q == 0):
                        pe.wait_ge(read, q)
                    for k in range(KT):
                        off = g * PC + k * P
                        last = three(ps[:, bank, :], lambda h: units[:, slot, h, off:off + P],
                                     lambda h: x1T[:, h, k, col(c * CH, CH)], k == 0, k == KT - 1)
                    last.then_inc(done, 1)

            def down(g, v, q, it, c):
                first, n = GROUPS[g]
                slot, r = slot_of(first + v), ring(v, n)
                pe.wait_ge(h_ready, q + 1)
                for s in range(SPC):
                    if v == 0:
                        pe.wait_ge(down_read, SPC * it + s + 1)
                    add_x1 = v == 0 and g == 0
                    if add_x1:
                        for k in range(KT):
                            for h in range(2):
                                mm(ps[:, DOWN + s, k * P:(k + 1) * P], x1T[:, h, k, col(c * CH + s * P, P)],
                                   ident64[:, :], start=(k == 0 and h == 0), stop=False)
                    last = three(ps[:, DOWN + s, :], lambda h: hffn[:, r, h, s * P:(s + 1) * P],
                                 lambda h: units[:, slot, h, 2 * PC:3 * PC], v == 0 and not add_x1, v == n - 1)
                    if v == n - 1:
                        last.then_inc(down_ps, 1)

            def body(g, c, peeled):
                first, n = GROUPS[g]
                q = tiles_before[g] + c * n
                it = NCH * g + c
                new, width = GROUPS[g + 1] if g + 1 < len(GROUPS) else (None, 0)
                for v in range(1, n + 1):
                    if v < n:
                        gate_up(first + v, q + v, c)
                    elif not peeled:
                        gate_up(first, q + n, c + 1)
                    elif new is not None:
                        gate_up(new, q + n, 0)
                    if new is not None and not (peeled and c >= width):
                        if v == 1:
                            unit_lora(new + c, (0, 1))
                        if v == (3 if n > 2 else 2):
                            unit_lora(new + c, (2,))
                    down(g, v - 1, q + v - 1, it, c)

            pe.wait_ge(x1_ready, 4 + 16)
            gate_up(0, 0, 0)
            for g in range(len(GROUPS)):
                with pe.Fori(0, NCH - 1) as c:
                    body(g, c, False)
                body(g, NCH - 1, True)


def kernel(**inputs):
    import numpy as np
    import concourse.bacc as bacc
    from concourse.bass_utils import run_bass_kernel_spmd

    a = {n: np.asarray(v) for n, v in inputs.items()}
    ca, sa = a["L0_attn_codes_attn"], a["L0_attn_scales_attn"]
    cg, sg = a["L0_attn_codes_gu"], a["L0_attn_scales_gu"]
    cd, sd = a["L0_attn_codes_down"], a["L0_attn_scales_down"]
    ah, ad = a["L0_attn_lora_A_h"], a["L0_attn_lora_A_down"]
    ba, bg, bd = a["L0_attn_lora_B_attn"], a["L0_attn_lora_B_gu"], a["L0_attn_lora_B_down"]

    codes4 = np.stack([ca[0], ca[1], ca[2], ca[3].T]).reshape(4, KT, P, D).transpose(1, 0, 2, 3)
    scales3 = sa[0:3].reshape(3, KT, P, NB).transpose(2, 1, 0, 3).reshape(P, KT, 3 * NB)
    scales_o = sa[3].T.reshape(KT, 2, D)
    cgt = cg.transpose(0, 2, 1).reshape(2, KT, P, UNITS, P).transpose(3, 0, 2, 1, 4).reshape(UNITS, 2, P, PC)
    cdt = cd.T.reshape(UNITS, 1, P, D)
    ucodes = np.concatenate([cgt, cdt], 1)
    sgt = sg.transpose(0, 2, 1).reshape(2, KT, 2, UNITS, P).transpose(3, 0, 2, 1, 4).reshape(UNITS, 2, 2, PC)
    sdt = sd.T.reshape(UNITS, 1, 2, D)
    uscales = np.concatenate([sgt, sdt], 1)
    pos = np.arange(T) % S
    share = np.stack([np.where(pos >= VISION, 1.0 / ((S - VISION) * D), 0.0),
                      np.where(pos < VISION, 1.0 / (VISION * D), 0.0)], -1).astype(np.float32)

    arrays = {
        "x": a["L0_attn_x"].reshape(T, D),
        "attn_codes": codes4, "attn_scales": scales3, "attn_scales_o": scales_o,
        "unit_codes": ucodes, "unit_scales": uscales,
        "lora_bt": ba[0:3].transpose(0, 2, 1).reshape(3 * R, KT, P).transpose(1, 0, 2),
        "lora_a": ah[0:3].reshape(3 * R, D),
        "lora_a3": ah[3].reshape(R, KT, P).transpose(1, 0, 2),
        "lora_bt3": ba[3].T,
        "lora_units": np.concatenate([ah[4:6].transpose(1, 0, 2).reshape(R, 2 * D), ad,
                                      bg.transpose(2, 0, 1).reshape(R, 2 * I), bd.T], 1),
        "gate_w": a["L0_ffn_gate_w"][0:D].reshape(KT, P, E).transpose(1, 0, 2),
        "gate_tail": a["L0_ffn_gate_w"][D:D + 1], "gate_b": a["L0_ffn_gate_b"].reshape(1, E),
        "w1": a["L0_ffn_w1"], "b1": a["L0_ffn_b1"].reshape(E, KT, P).transpose(0, 2, 1),
        "w2": a["L0_ffn_w2"], "b2": a["L0_ffn_b2"],
        "eye": np.eye(P, dtype=np.float32),
        "region": share.reshape(NST, P, 2).transpose(1, 0, 2),
    }
    arrays = {f"in_{n}": np.ascontiguousarray(v) for n, v in arrays.items()}
    nc = bacc.Bacc("TRN2", target_bir_lowering=False, num_devices=1)
    args = {n[3:]: nc.dram_tensor(n, v.shape, mybir.dt.from_np(v.dtype), kind="ExternalInput").ap()
            for n, v in arrays.items()}
    args["m_store"] = nc.dram_tensor("m_store", (B, NST // B, P, D), F32, kind="Internal").ap()
    args["out"] = nc.dram_tensor("out", (T, D), F32, kind="ExternalOutput").ap()
    build(nc, **args)
    r = run_bass_kernel_spmd(nc, [arrays], core_ids=[0])
    return r.results[0]["out"].reshape(B, S, D)
```

```python
from contextlib import ExitStack

import numpy as np
import concourse.bass as bass
from concourse import mybir

F32 = mybir.dt.float32
F16 = mybir.dt.float16
I32 = mybir.dt.int32
ALU = mybir.AluOpType
ACT = mybir.ActivationFunctionType

NF4 = [-1.0, -0.6961928009986877, -0.5250730514526367, -0.39491748809814453, -0.28444138169288635,
       -0.18477343022823334, -0.09105003625154495, 0.0, 0.07958029955625534, 0.16093020141124725,
       0.24611230194568634, 0.33791524171829224, 0.44070982933044434, 0.5626170039176941,
       0.7229568362236023, 1.0]

P = 128
B, S, D = 2, 1024, 512
T = B * S
KT = D // P
NST = T // P
CH = 512
NCH = T // CH
SPC = CH // P
I = 1792
UNITS = I // P
R = 16
E = 3
NB = D // 64
PC = 512
WS = 64.0
AS, BS = 16.0, 4.0
EPS = 1e-5
VISION = int(S * 0.3)
GROUPS = [(0, 3), (3, 4), (7, 4), (11, 3)]
X_LOADS = [(t, 1) for t in range(8)] + [(8, 4), (12, 4)]
SLOTS = 8
ROT = 5


def slot_of(u):
    return (u + ROT) % SLOTS


def nf4_terms():
    ramps, corner = [(1, 7), (4, 9), (6, 11), (10, 13)], 2
    a = np.zeros((15, 15))
    a[:, 0] = 1.0
    for n, (first, last) in enumerate(ramps):
        a[first + 1:last, 1 + 3 * n] = -1.0
        a[first, 2 + 3 * n] = -1.0
        a[last, 3 + 3 * n] = -1.0
    a[corner + 1:, 13] = -1.0
    a[corner, 14] = -1.0
    u = np.linalg.solve(a, np.diff(NF4))
    start = corner + 1 - u[14] / u[13]
    terms, caps = [(float(u[13]), float(-u[13] * start))], []
    for n, (first, last) in enumerate(ramps):
        slope, rise0, rise1 = u[1 + 3 * n:4 + 3 * n]
        start, end = first + 1 - rise0 / slope, last + rise1 / slope
        terms.append((float(slope), float(-slope * start)))
        caps.append(float(slope * (end - start)))
    return float(u[0]), terms, caps


NF4_SLOPE, NF4_TERMS, NF4_CAPS = nf4_terms()
NTERM = len(NF4_TERMS)
ADDS = NTERM
READ_BY = [1, 1, 2, 3, 4]
SCALE, LORA, LOW = 6, 7, 8
HIGH = 8


def build(nc, x, attn_codes, attn_scales, attn_scales_o, unit_codes, unit_scales, lora_bt, lora_a,
          lora_a3, lora_bt3, lora_units, gate_w, gate_tail, gate_b, w1, b1, w2, b2,
          eye, region, m_store, out):
    ctx = ExitStack()
    with ctx:
        def sb(name, shape, dt):
            return ctx.enter_context(nc.sbuf_tensor(name, shape, dt))

        def sem(name):
            return ctx.enter_context(nc.semaphore(name))

        reg_a = sb("reg_a", [P, NST * D], F32)
        xnT = reg_a[:, :].bitcast(F16).rearrange("p (h k t) -> p h k t", h=2, k=KT)
        acc = reg_a[:, :].rearrange("p (s d) -> p s d", d=D)
        reg_b = sb("reg_b", [P, NST * D], F32)
        xs = reg_b[:, :].rearrange("p (s d) -> p s d", d=D)
        wpair = reg_b[:, 4096:8192].bitcast(F16).rearrange("p (w h k f) -> p w h k f", w=2, h=2, k=KT)
        wstage = reg_b[:, 0:4096].rearrange("p (w n) -> p w n", w=2)
        x1T = reg_b[:, :].bitcast(F16).rearrange("p (h k t) -> p h k t", h=2, k=KT)
        reg_c = sb("reg_c", [P, SLOTS * 3 * PC], F32)
        units = reg_c[:, :].bitcast(F16).rearrange("p (s h n) -> p s h n", s=SLOTS, h=2)
        mix = reg_c[:, 0:4096].rearrange("p (s d) -> p s d", d=D)
        NRAW = 2 * D + I + 2 * I + D
        raw = reg_c[:, 4096:4096 + NRAW]
        L0 = 4096 + NRAW
        la = reg_c[:, L0:L0 + D]
        lb = reg_c[:, L0 + D:L0 + D + P]
        b2p = reg_c[:, L0 + D + P:L0 + 2 * D + P].bitcast(F16).rearrange("p (s n) -> p s n", s=2)
        assert L0 + 2 * D + P <= SLOTS * 3 * PC
        reg_d = sb("reg_d", [P, 4096], F32)
        hmix = reg_d[:, :].bitcast(F16).rearrange("p (c h f t) -> p c h f t", c=2, h=2, f=KT)
        hffn = reg_d[:, 0:3 * CH].bitcast(F16).rearrange("p (r h t) -> p r h t", r=3, h=2)
        sgate = reg_d[:, 3 * CH:6 * CH].rearrange("p (r t) -> p r t", r=3)
        h32 = reg_d[:, 6 * CH:8 * CH].rearrange("p (r t) -> p r t", r=2)
        act32 = sb("act32", [P, 2, CH], F32)
        reg_e = sb("reg_e", [P, 2 * KT * D], F32)
        wa = reg_e[:, 0:KT * D].rearrange("p (k n) -> p k n", k=KT)
        w3 = reg_e[:, KT * D:2 * KT * D].rearrange("p (k n) -> p k n", k=KT)
        fin_g = reg_e[:, 0:SPC * D].rearrange("p (s d) -> p s d", s=SPC)
        fin_x = reg_e[:, SPC * D:2 * SPC * D].rearrange("p (s d) -> p s d", s=SPC)
        last_g = reg_c[:, 4 * 3 * PC:4 * 3 * PC + SPC * D].rearrange("p (s d) -> p s d", s=SPC)
        last_x = reg_c[:, 4 * 3 * PC + SPC * D:4 * 3 * PC + 2 * SPC * D].rearrange("p (s d) -> p s d", s=SPC)
        cpair = sb("cpair", [P, 2, KT, D], F16)
        stack = sb("stack", [P, NRAW], F16)
        s_au = stack[:, 0:2 * D].rearrange("p (g n) -> p g n", g=2)
        s_ad = stack[:, 2 * D:2 * D + I]
        s_bu = stack[:, 2 * D + I:2 * D + 3 * I].rearrange("p (g n) -> p g n", g=2)
        s_bd = stack[:, 2 * D + 3 * I:NRAW]
        STACK_PARTS = [(0, 2 * D + I, AS), (2 * D + I, 2 * I + D, BS)]
        codes = sb("codes", [P, 4, PC], I32)
        scl = sb("scl", [P, 3, PC], F32)
        term = sb("term", [P, NTERM, PC], F32)
        suma = sb("suma", [P, 3, PC], F32)
        tbias = sb("tbias", [P, 2, NTERM], F32)
        ascl = sb("ascl", [P, KT, 3 * NB], F32)
        b2r = scl[:, 1:3, :]
        ident = sb("ident", [P, P], F32)
        ident3 = sb("ident3", [P, P], F32)
        ident64 = sb("ident64", [P, P], F16)
        ones = sb("ones", [P, P], F32)
        ones16 = sb("ones16", [P, P], F16)
        share = sb("share", [P, NST, 2], F32)
        shared_abs = sb("shared_abs", [P, NST, 2], F32)
        abs_part = sb("abs_part", [P, B, 2], F32)
        bst = sb("bst", [P, NST, 6], F32)
        mv = sb("mv", [P, NST, 2], F32)
        std = sb("std", [P, NST], F32)
        rstd = sb("rstd", [P, NST], F32)
        epst = sb("epst", [P, 1], F32)
        absum = sb("absum", [P, NST], F32)
        gw = sb("gw", [P, KT, E], F32)
        gw6 = sb("gw6", [P, KT, 2 * E], F16)
        gtail = sb("gtail", [P, 2, E], F32)
        strength = sb("strength", [P, B, 2], F32)
        ratio = sb("ratio", [P, B], F32)
        addl = sb("addl", [P, B, E], F32)
        lgt = sb("lgt", [P, NST, E], F32)
        lgs = sb("lgs", [P, NST, E], F32)
        pr = sb("pr", [P, NST, E], F32)
        rt = sb("rt", [P, 8, NST], F32)
        coef = sb("coef", [P, B, 2, NST // B], F32)
        rk = sb("rk", [1, 12, B], F32)
        idx = sb("idx", [1, 8], I32)
        b1t = sb("b1t", [P, 2, KT], F32)

        ps = ctx.enter_context(nc.psum_tensor("ps", [P, 8, 512], F32))
        PRE, OUT, ABA, UBA, GATE, UP, DOWN = 0, 2, 4, 6, 0, 1, 2
        TBANKS, ROUTER = 6, 6
        STRENGTH = 128

        x_in = [sem(f"x_in{q}") for q in range(len(X_LOADS))]
        eye_in = sem("eye_in")
        router_in = sem("router_in")
        attn_in = sem("attn_in")
        raw_zero = sem("raw_zero")
        raw_in = sem("raw_in")
        stack_hi = sem("stack_hi")
        stacks_ready = sem("stacks_ready")
        setup_done = sem("setup_done")
        ident_ready = sem("ident_ready")
        stats_step = sem("stats_step")
        stats_ready = sem("stats_ready")
        std_ready = sem("std_ready")
        rstd_ready = sem("rstd_ready")
        xn_ready = sem("xn_ready")
        abs_done = sem("abs_done")
        xt_ps = sem("xt_ps")
        xt_hi = sem("xt_hi")
        xt_lo = sem("xt_lo")
        gw_ready = sem("gw_ready")
        abs_ready = sem("abs_ready")
        router_ps = sem("router_ps")
        rt_step = sem("rt_step")
        lgs_ready = sem("lgs_ready")
        exp_ready = sem("exp_ready")
        idx_ready = sem("idx_ready")
        w_in = [sem(f"w{w + 1}_in") for w in range(2)]
        w_hi = [sem(f"w{w + 1}_hi") for w in range(2)]
        w_ready = [sem(f"w{w + 1}_ready") for w in range(2)]
        b1_in = [sem(f"b1_in{r}") for r in range(2)]
        b2_in = [sem(f"b2_in{r}") for r in range(2)]
        b2_hi = sem("b2_hi")
        b2_ready = sem("b2_ready")
        pre_ps = sem("pre_ps")
        act_ready = sem("act_ready")
        hmix_ready = sem("hmix_ready")
        out_ps = sem("out_ps")
        out0_read = sem("out0_read")
        out1_read = sem("out1_read")
        mix_stored = sem("mix_stored")
        mix_free = sem("mix_free")
        acodes_in = [sem(f"acodes_in{k}") for k in range(4)]
        ascl_in = sem("ascl_in")
        lb_in = sem("lb_in")
        aterm = sem("aterm")
        aread = sem("aread")
        ascaled = sem("ascaled")
        amerged = sem("amerged")
        aba_ps = sem("aba_ps")
        c_ps = sem("c_ps")
        c_hi = sem("c_hi")
        c_ready = sem("c_ready")
        x1_ps = sem("x1_ps")
        x1_hi = sem("x1_hi")
        x1_ready = sem("x1_ready")
        ucodes_in = [sem(f"ucodes_in{k}") for k in range(3)]
        uscl_in = [sem(f"uscl_in{k}") for k in range(3)]
        uterm = sem("uterm")
        uread = sem("uread")
        uscaled = sem("uscaled")
        usum = sem("usum")
        uhi = sem("uhi")
        uready = sem("uready")
        uba_ps = sem("uba_ps")
        gate_ps = sem("gate_ps")
        up_ps = sem("up_ps")
        silu_done = sem("silu_done")
        h_ready32 = sem("h_ready32")
        h_hi = sem("h_hi")
        h_ready = sem("h_ready")
        down_ps = sem("down_ps")
        down_read = sem("down_read")
        fm_in = [sem(f"fm_in{s}") for s in range(SPC)]
        fx_in = [sem(f"fx_in{s}") for s in range(SPC)]
        lm_in = sem("lm_in")
        lx_in = sem("lx_in")
        fgate = sem("fgate")
        fscaled = sem("fscaled")
        fbase = sem("fbase")
        fout = sem("fout")
        stored = [sem(f"stored{s}") for s in range(SPC)]

        block = ctx.enter_context(nc.Block())

        def dealt(seq, weights):
            ends = [round(len(seq) * sum(weights[:i]) / sum(weights)) for i in range(len(weights) + 1)]
            return [seq[a:b] for a, b in zip(ends, ends[1:])]

        def followed(sca_seq, vec_parts):
            at, parts, done = {step: i for i, step in enumerate(sca_seq)}, [], 0
            steps = [s for vec in vec_parts for s in vec]
            seen = 0
            for vec in vec_parts:
                seen += len(vec)
                for k, n in steps[:seen + 1]:
                    if n <= ADDS or n == LOW:
                        done = max(done, at[k, min(n, NTERM - 1) if n <= ADDS else HIGH] + 1)
                parts.append(sca_seq[sum(map(len, parts)):done])
            return parts

        VEC_SEQ, SCA_SEQ = [], []
        for k in range(3):
            after = [(k - 1, n) for n in (SCALE, LORA, LOW)] if k else []
            VEC_SEQ += [(k, 1)] + after[0:1] + [(k, 2)] + after[1:2] + [(k, 3), (k, 4)] + after[2:3] + [(k, 5)]
            SCA_SEQ += [(k, e) for e in range(NTERM)] + ([(k - 1, HIGH)] if k else [])
        VEC_SEQ += [(2, SCALE), (2, LORA), (2, LOW)]
        SCA_SEQ += [(2, HIGH)]
        VEC_UNIT0 = dealt(VEC_SEQ, (5, 4, 5, 3, 7))
        SCA_UNIT0 = followed(SCA_SEQ, VEC_UNIT0)
        VEC_UNIT = {n: dealt(VEC_SEQ, [1] * n) for n in (3, 4, 8)}
        SCA_UNIT = {n: followed(SCA_SEQ, VEC_UNIT[n]) for n in VEC_UNIT}
        FINAL_AT = [{1: (), 2: (0, 1), 3: (2, 3)}, {1: (0, 1, 2), 2: (3,), 3: ()}]
        VEC_ATTN, SCA_ATTN = [], []
        for k in range(4):
            after = [(k - 1, n) for n in (SCALE, LORA)] if k else []
            VEC_ATTN += [(k, 1)] + after[0:1] + [(k, 2)] + after[1:2] + [(k, n) for n in (3, 4, 5)]
            SCA_ATTN += [(k, e) for e in range(NTERM)]
        VEC_ATTN += [(3, SCALE), (3, LORA)]
        ATTN_WEIGHTS = [5] * 8 + [7] * 5 + [0] * 3
        VEC_ATTN = dealt(VEC_ATTN, ATTN_WEIGHTS)
        SCA_ATTN = followed(SCA_ATTN, VEC_ATTN)

        tiles_before = [NCH * sum(n for _, n in GROUPS[:g]) for g in range(len(GROUPS))]

        def ring(v, n):
            return v % n % (3 if n % 2 else 2)

        def col(v, n):
            return slice(v, v + n) if isinstance(v, int) else bass.ds(v, n)

        @block.sync
        def _(sp):
            for q, (t, n) in enumerate(X_LOADS):
                sp.dma_start(xs[:, t:t + n, :], x[t * P:(t + n) * P, :].rearrange("(s p) d -> p s d", p=P)).then_inc(x_in[q], 16)
                if t == 5:
                    sp.dma_start(ident[:, :], eye).then_inc(eye_in, 16)
                if t == 7:
                    for dst, src in ((gw[:, :, :], gate_w), (share[:, :, :], region), (gtail[:, 0, :], gate_tail.to_broadcast([P, E])),
                                     (gtail[:, 1, :], gate_b.to_broadcast([P, E]))):
                        sp.dma_start(dst, src).then_inc(router_in, 16)
            for dst, src in ((ascl[:, :, :], attn_scales), (la[0:3 * R, :], lora_a), (la[64:64 + R, :], lora_bt3)):
                sp.dma_start(dst, src).then_inc(attn_in, 16)
            sp.wait_ge(setup_done, 2)

            def load_attn(n):
                for k in range(4):
                    sp.wait_ge(amerged, 4 * n + k + 1)
                    sp.dma_start(codes[:, k, :],
                                 attn_codes[col(n, 1), k, :, :].rearrange("a p c -> p (a c)")).then_inc(acodes_in[k], 16)
                sp.dma_start(lb[0:3 * R, :], lora_bt[col(n, 1), :, :].rearrange("a r m -> r (a m)")).then_inc(lb_in, 16)
                sp.dma_start(lb[64:64 + R, :], lora_a3[col(n, 1), :, :].rearrange("a r m -> r (a m)")).then_inc(lb_in, 16)
                for half in range(2):
                    sp.dma_start(scl[64 * half:64 * half + 64, 0, :],
                                 attn_scales_o[col(n, 1), half, :].to_broadcast([64, PC])).then_inc(ascl_in, 16)

            def load_w(n, w, slot):
                j = sp.value_load(idx[0:1, col(n, 1)], min_val=0, max_val=E - 1)
                sp.wait_ge(w_ready[w], n + 1)
                if w == 0:
                    sp.dma_start(b1t[:, slot, :], b1[bass.ds(j, 1), :, :].rearrange("a p k -> p (a k)")).then_inc(b1_in[slot], 16)
                else:
                    for row in (0, 32):
                        sp.dma_start(b2r[row:row + 1, slot, :], b2[bass.ds(j, 1), :]).then_inc(b2_in[slot], 16)
                sp.dma_start(wstage[:, w, :].rearrange("p (k f) -> p k f", k=KT),
                             (w1, w2)[w][bass.ds(j, 1), :, :].rearrange("a (k p) f -> p (a k) f", p=P)).then_inc(w_in[w], 16)

            for b in range(B):
                for slot in range(2):
                    sp.wait_ge(idx_ready, 2 * b + slot + 1)
                    load_w(2 * b + slot, 0, slot)
                    load_w(2 * b + slot, 1, slot)
                    load_attn(2 * b + slot)
            load_w(2 * B, 0, 0)

            sp.wait_ge(amerged, 4 * 4 + 4)
            sp.wait_ge(b2_ready, 2 * B)
            with sp.Fori(0, UNITS) as u:
                for k in range(3):
                    sp.wait_ge(usum, 3 * u + k + 1)
                    sp.dma_start(codes[:, k, :],
                                 unit_codes[bass.ds(u, 1), k, :, :].rearrange("a p c -> p (a c)")).then_inc(ucodes_in[k], 16)
                    for half in range(2):
                        sp.dma_start(scl[64 * half:64 * half + 64, k, :],
                                     unit_scales[bass.ds(u, 1), k, half, :].to_broadcast([64, PC])).then_inc(uscl_in[k], 16)

            sp.wait_ge(c_ready, KT)
            sp.wait_ge(mix_stored, 16 * B)

            def load_m(t, s):
                sp.dma_start(fin_g[:, s, :], m_store.rearrange("b s p d -> (b s) p d")[col(t, 1), :, :].rearrange("a p d -> p (a d)")).then_inc(fm_in[s], 16)

            def load_x_again(t, s):
                sp.dma_start(fin_x[:, s, :], x.rearrange("(s p) d -> s p d", p=P)[col(t, 1), :, :].rearrange("a p d -> p (a d)")).then_inc(fx_in[s], 16)

            def store(t, s, source):
                sp.wait_ge(fout, t + 1)
                sp.dma_start(out.rearrange("(s p) d -> s p d", p=P)[col(t, 1), :, :].rearrange("a p d -> p (a d)"),
                             source[:, s, :]).then_inc(stored[s], 16)

            for s in range(SPC):
                load_m(s, s)
                load_x_again(s, s)
            sp.wait_ge(down_ps, SPC * NCH * (len(GROUPS) - 1))
            sp.dma_start(last_g, m_store.rearrange("b s p d -> p (b s) d")[:, NST - SPC:NST, :]).then_inc(lm_in, 16)
            sp.dma_start(last_x, x[T - CH:T, :].rearrange("(s p) d -> p s d", p=P)).then_inc(lx_in, 16)
            with sp.Fori(0, NCH - 2) as c:
                for s in range(SPC):
                    store(SPC * c + s, s, fin_x)
                    load_m(SPC * c + s + SPC, s)
                for s in range(SPC):
                    sp.wait_ge(stored[s], 16 * c + 16)
                    load_x_again(SPC * c + s + SPC, s)
            for c, source in ((NCH - 2, fin_x), (NCH - 1, last_x)):
                for s in range(SPC):
                    store(SPC * c + s, s, source)
            for s in range(SPC):
                sp.wait_ge(stored[s], 16 * NCH)

        @block.gpsimd
        def _(gp):
            nc.gpsimd.memset(raw, 0.0).then_inc(raw_zero, 1)
            gp.wait_ge(raw_zero, 1)
            for q in range(4):
                gp.dma_start(raw[32 * q:32 * q + R, :], lora_units).then_inc(raw_in, 16)
            gp.sem_inc(mix_free, 1)
            with gp.Fori(0, B) as b:
                gp.wait_ge(out1_read, 8 * b + 16)
                gp.dma_start(m_store[bass.ds(b, 1), :, :, :].rearrange("a s p d -> p (a s) d"), mix).then_inc(mix_stored, 16)
                gp.wait_ge(mix_stored, 16 * b + 16)
                gp.sem_inc(mix_free, 1)

        @block.scalar
        def _(act):
            act.wait_ge(setup_done, 2)

            def stds(b):
                s0 = b * NST // B
                act.wait_ge(stats_ready, (b + 1) * NST // B)
                nc.scalar.activation(std[:, s0:s0 + NST // B], mv[:, s0:s0 + NST // B, 1], ACT.Sqrt,
                                     bias=epst[:, 0:1]).then_inc(std_ready, 1)

            def token_tiles(t0, t1):
                for t in range(t0, t1):
                    act.wait_ge(xn_ready, t + 1)
                    if t >= NTERM:
                        act.wait_ge(abs_done, t - NTERM + 1)
                    nc.scalar.activation(term[:, t % NTERM, :], xs[:, t, :], ACT.Abs, accum_out=absum[:, t:t + 1]).then_inc(abs_done, 1)
                    act.wait_ge(xt_ps, t + 1)
                    nc.scalar.activation(xnT[:, 0, :, t * P:(t + 1) * P],
                                         ps[:, t % TBANKS, :].rearrange("p (k t) -> p k t", k=KT), ACT.Copy).then_inc(xt_hi, 1)

            def nf4_term(e, codes_k, ws, done):
                nc.scalar.activation(term[:, e, :], codes_k, ACT.Relu, bias=tbias[:, ws, e:e + 1],
                                     scale=NF4_TERMS[e][0] * (WS if ws else 1.0)).then_inc(done, 1)

            def attn_term(n, k, e):
                if e == 0:
                    act.wait_ge(acodes_in[k], 16 * n + 16)
                act.wait_ge(aread, ADDS * (4 * n + k) + READ_BY[e])
                nf4_term(e, codes[:, k, :], 0, aterm)

            def w_high(w):
                nc.scalar.activation(wpair[:, w, 0, :, :], wstage[:, w, :].rearrange("p (k f) -> p k f", k=KT),
                                     ACT.Copy, scale=WS).then_inc(w_hi[w], 1)

            def stack_high(c0, width, scale):
                act.wait_ge(raw_in, 16 * 4)
                nc.scalar.activation(stack[:, c0:c0 + width], raw[:, c0:c0 + width], ACT.Copy, scale=scale).then_inc(stack_hi, 1)

            act.sem_inc(act_ready, 2)
            stds(0)
            token_tiles(0, 8)
            stds(1)
            stack_high(*STACK_PARTS[0])
            token_tiles(8, 13)
            act.wait_ge(abs_done, 12)
            act.wait_ge(w_in[0], 16)
            w_high(0)
            token_tiles(13, 16)
            act.wait_ge(abs_done, NST)
            stack_high(*STACK_PARTS[1])
            act.wait_ge(lgs_ready, 1)
            nc.scalar.activation(pr[:, :, :], lgs[:, :, :], ACT.Exp).then_inc(exp_ready, 1)
            act.wait_ge(idx_ready, 2 * B)
            with act.Fori(0, B) as b:
                for slot in range(2):
                    n = 2 * b + slot
                    j = act.value_load(idx[0:1, bass.ds(n, 1)], min_val=0, max_val=E - 1)
                    for expert, func in ((0, ACT.Tanh), (1, ACT.Gelu), (2, ACT.Silu)):
                        with act.If(j == expert):
                            act.wait_ge(b1_in[slot], 16 * b + 16)
                            for t in range(2 * KT):
                                c, f = t // KT, t % KT
                                act.wait_ge(pre_ps, 8 * n + t + 1)
                                act.wait_ge(hmix_ready, 8 * n + t + 1)
                                nc.scalar.activation(act32[:, t % 2, :], ps[:, PRE + t % 2, :], func,
                                                     bias=b1t[:, slot, f:f + 1], scale=1.0 / WS)
                                nc.scalar.activation(hmix[:, c, 0, f, :], ps[:, PRE + t % 2, :], func,
                                                     bias=b1t[:, slot, f:f + 1], scale=1.0 / WS).then_inc(act_ready, 1)
                                if t == 0:
                                    act.wait_ge(w_in[1], 16 * n + 16)
                                    w_high(1)
                                for k, e in SCA_ATTN[t]:
                                    attn_term(n, k, e)
                    for s in range(8):
                        if s == 2:
                            act.wait_ge(w_in[0], 16 * n + 32)
                            w_high(0)
                        if slot == 0:
                            if s == 0:
                                act.wait_ge(mix_free, b + 1)
                            act.wait_ge(out_ps, 8 * n + s + 1)
                            nc.scalar.activation(mix[:, s, :], ps[:, OUT + s % 2, :], ACT.Copy,
                                                 scale=coef[:, bass.ds(b, 1), 0, s]).then_inc(out0_read, 1)
                        for k, e in SCA_ATTN[8 + s]:
                            attn_term(n, k, e)

            def unit_step(u, slot, k, e):
                p = 3 * u + k
                if e == HIGH:
                    act.wait_ge(usum, p + 4)
                    nc.scalar.activation(units[:, col(slot, 1), 0, k * PC:(k + 1) * PC].rearrange("p a n -> p (a n)"),
                                         suma[:, k, :], ACT.Copy).then_inc(uhi, 1)
                    return
                if e == 0:
                    act.wait_ge(ucodes_in[k], 16 * u + 16)
                act.wait_ge(uread, ADDS * p + READ_BY[e])
                nf4_term(e, codes[:, k, :], 1, uterm)

            for k in range(KT):
                for piece, e in SCA_UNIT0[k]:
                    unit_step(0, slot_of(0), piece, e)
                act.wait_ge(c_ps, k + 1)
                nc.scalar.activation(cpair[:, 0, k, :], ps[:, k, :], ACT.Copy, scale=WS / 3.0).then_inc(c_hi, 1)
            for piece, e in SCA_UNIT0[KT]:
                unit_step(0, slot_of(0), piece, e)

            with act.Fori(0, 2) as i:
                for t in range(8):
                    c, o = t // KT, t % KT
                    act.wait_ge(x1_ps, 8 * i + t + 1)
                    nc.scalar.activation(x1T[:, 0, o, bass.ds(i * (2 * CH) + c * CH, CH)], ps[:, t % 4, :], ACT.Copy,
                                         scale=1.0 / WS).then_inc(x1_hi, 1)
                    for k, e in SCA_UNIT[8][t]:
                        unit_step(i + 1, i + slot_of(1), k, e)

            def silu(q, r):
                act.wait_ge(gate_ps, q + 1)
                nc.scalar.activation(sgate[:, r, :], ps[:, GATE, :], ACT.Silu, scale=1.0 / WS).then_inc(silu_done, 1)

            def high(q, r):
                act.wait_ge(h_ready32, q + 1)
                nc.scalar.activation(hffn[:, r, 0, :], h32[:, r % 2, :], ACT.Copy).then_inc(h_hi, 1)

            def body(g, c, last):
                first, n = GROUPS[g]
                q = tiles_before[g] + c * n
                it = NCH * g + c
                new, width = GROUPS[g + 1] if g + 1 < len(GROUPS) else (None, 0)
                for v in range(1, n + 1):
                    steps = SCA_UNIT[n][v - 1] if new is not None and not (isinstance(c, int) and c >= width) else []
                    early = 0
                    while early < min(2, len(steps)) and steps[early][1] != HIGH:
                        early += 1
                    if not (last and v == n):
                        silu(q + v, ring(v, n))
                    for k, e in steps[:early]:
                        unit_step(new + c, slot_of(new) + c, k, e)
                    if not (last and v == n):
                        high(q + v, ring(v, n))
                    for k, e in steps[early:]:
                        unit_step(new + c, slot_of(new) + c, k, e)
                    if new is None:
                        for s in FINAL_AT[last][v]:
                            if last:
                                act.wait_ge(lm_in, 16)
                            else:
                                act.wait_ge(fm_in[s], 16 * c + 16)
                            gate = (last_g if last else fin_g)[:, s, :]
                            nc.scalar.activation(gate, gate, ACT.Silu).then_inc(fgate, 1)
                if g == 0:
                    for s in range(SPC):
                        act.wait_ge(down_ps, SPC * it + s + 1)
                        nc.scalar.activation(acc[:, col(SPC * c + s, 1), :].rearrange("p a d -> p (a d)"), ps[:, DOWN + s, :],
                                             ACT.Copy).then_inc(down_read, 1)

            act.wait_ge(mix_free, B + 1)
            silu(0, 0)
            high(0, 0)
            for g in range(len(GROUPS)):
                with act.Fori(0, NCH - 1) as c:
                    body(g, c, False)
                body(g, NCH - 1, g == len(GROUPS) - 1)

        @block.vector
        def _(vec):
            vector = nc.vector
            for e, (_, bias) in enumerate(NF4_TERMS):
                vector.memset(tbias[:, 0, e:e + 1], bias)
                vector.memset(tbias[:, 1, e:e + 1], bias * WS)
            vector.memset(epst[:, :], EPS)
            vector.memset(ones[:, :], 1.0)
            vector.memset(ones16[:, :], 1.0).then_inc(setup_done, 1)
            vector.memset(idx[:, :], 0)
            vector.memset(b2r, 0.0).then_inc(setup_done, 1)
            vec.sem_inc(hmix_ready, 2)
            vec.sem_inc(out1_read, 8)
            vec.sem_inc(aread, ADDS)
            vec.sem_inc(amerged, 4)
            vec.sem_inc(uread, ADDS)
            vec.sem_inc(usum, 3)
            vec.sem_inc(x1_ready, 4)
            vec.sem_inc(down_read, 4)
            for w in range(2):
                vec.sem_inc(w_ready[w], 1)

            arrives = {t: q for q, (t, _) in enumerate(X_LOADS)}

            def stats(t):
                if t in arrives:
                    vec.wait_ge(x_in[arrives[t]], 16)
                vector.bn_stats(bst[:, t, :], xs[:, t, :]).then_inc(stats_step, 1)

            def aggregate(b):
                for t in range(b * NST // B, (b + 1) * NST // B):
                    vec.wait_ge(stats_step, t + 1)
                    vector.bn_aggr(mv[:, t, :], bst[:, t, :]).then_inc(stats_ready, 1)

            def normalise(b):
                vec.wait_ge(std_ready, b + 1)
                t0, t1 = b * NST // B, (b + 1) * NST // B
                vector.reciprocal(rstd[:, t0:t1], std[:, t0:t1]).then_inc(rstd_ready, 1)
                vec.wait_ge(rstd_ready, b + 1)
                for t in range(t0, t1):
                    vector.tensor_scalar(xs[:, t, :], xs[:, t, :], mv[:, t, 0:1], rstd[:, t:t + 1], ALU.subtract,
                                         ALU.mult).then_inc(xn_ready, 1)

            def token_low(t0, t1):
                for t in range(t0, t1):
                    vec.wait_ge(xt_hi, t + 1)
                    vector.tensor_tensor(xnT[:, 1, :, t * P:(t + 1) * P], ps[:, t % TBANKS, :].rearrange("p (k t) -> p k t", k=KT),
                                         xnT[:, 0, :, t * P:(t + 1) * P], ALU.subtract).then_inc(xt_lo, 1)

            linked = [0]

            def link(ins):
                linked[0] += 1
                ins.then_inc(rt_step, 1)
                vec.wait_ge(rt_step, linked[0])

            def abs_sums(b):
                t0, t1 = b * NST // B, (b + 1) * NST // B
                vec.wait_ge(abs_done, t1)
                link(vector.tensor_tensor(shared_abs[:, t0:t1, :], share[:, t0:t1, :],
                                          absum[:, t0:t1].unsqueeze(2).to_broadcast([P, NST // B, 2]), ALU.mult))
                vector.tensor_reduce(abs_part[:, b, :], shared_abs[:, t0:t1, :].rearrange("p s r -> p r s"),
                                     mybir.AxisListType.X, ALU.add).then_inc(abs_ready, 1)

            def router(b):
                t0, t1 = b * NST // B, (b + 1) * NST // B
                n = NST // B
                lg, ls = lgt[:, t0:t1, :], lgs[:, t0:t1, :]
                vec.wait_ge(router_ps, b + 1)
                raw_logits = ps[:, ROUTER + b, 0:2 * E * n].rearrange("p (t e) -> p t e", e=2 * E)
                link(vector.tensor_copy(strength[:, b, :], ps[:, ROUTER + b, STRENGTH:STRENGTH + 2]))
                vector.tensor_copy(ls, raw_logits[:, :, E:2 * E])
                link(vector.tensor_scalar(ratio[:, b:b + 1], strength[:, b, 1:2], 1e-8, None, ALU.add))
                vector.tensor_tensor(lg, raw_logits[:, :, 0:E], ls, ALU.add)
                link(vector.reciprocal(ratio[:, b:b + 1], ratio[:, b:b + 1]))
                link(vector.tensor_tensor(ratio[:, b:b + 1], ratio[:, b:b + 1], strength[:, b, 0:1], ALU.mult))
                link(vector.scalar_tensor_tensor(addl[:, b, :], gtail[:, 0, :], ratio[:, b:b + 1], gtail[:, 1, :], ALU.mult, ALU.add))
                link(vector.scalar_tensor_tensor(lg, lg, 1.0 / WS, addl[:, b:b + 1, :].to_broadcast([P, n, E]), ALU.mult, ALU.add))
                first = [lgt[0:1, t0, e:e + 1] for e in range(E)]
                k = rk[:, :, b:b + 1]
                for row, a, b_, op in ((0, 1, 0, ALU.is_gt), (1, 2, 0, ALU.is_gt), (2, 0, 1, ALU.is_ge),
                                       (3, 2, 1, ALU.is_gt), (4, 0, 2, ALU.is_ge), (5, 1, 2, ALU.is_ge)):
                    last = vector.tensor_tensor(k[:, row, :], first[a], first[b_], op)
                link(last)
                for e in (1, 2):
                    last = vector.tensor_tensor(k[:, 6 + e, :], k[:, 2 * e, :], k[:, 2 * e + 1, :], ALU.add)
                link(last)
                for choice in range(2):
                    vector.tensor_scalar(k[:, 9, :], k[:, 7, :], float(choice), None, ALU.is_equal)
                    link(vector.tensor_scalar(k[:, 10, :], k[:, 8, :], float(choice), 2.0, ALU.is_equal, ALU.mult))
                    link(vector.tensor_tensor(k[:, 11, :], k[:, 9, :], k[:, 10, :], ALU.add))
                    vector.tensor_scalar(idx[:, 2 * b + choice:2 * b + choice + 1], k[:, 11, :], float(E - 1), None,
                                         ALU.min).then_inc(idx_ready, 1)

            def coefficients():
                link(vector.tensor_tensor(rt[:, 0, :], lgt[:, :, 0], lgt[:, :, 1], ALU.max))
                link(vector.tensor_tensor(rt[:, 0, :], rt[:, 0, :], lgt[:, :, 2], ALU.max))
                vector.tensor_tensor(lgs[:, :, :], lgt[:, :, :], rt[:, 0, :].unsqueeze(2).to_broadcast([P, NST, E]),
                                     ALU.subtract).then_inc(lgs_ready, 1)
                vec.wait_ge(exp_ready, 1)
                link(vector.tensor_tensor(rt[:, 1, :], pr[:, :, 0], pr[:, :, 1], ALU.add))
                link(vector.tensor_tensor(rt[:, 1, :], rt[:, 1, :], pr[:, :, 2], ALU.add))
                link(vector.reciprocal(rt[:, 1, :], rt[:, 1, :]))
                link(vector.tensor_tensor(pr[:, :, :], pr[:, :, :], rt[:, 1, :].unsqueeze(2).to_broadcast([P, NST, E]), ALU.mult))
                vector.tensor_tensor(rt[:, 2, :], pr[:, :, 0], pr[:, :, 1], ALU.max)
                link(vector.tensor_tensor(rt[:, 3, :], pr[:, :, 0], pr[:, :, 1], ALU.min))
                vector.tensor_tensor(rt[:, 4, :], rt[:, 2, :], pr[:, :, 2], ALU.max)
                link(vector.tensor_tensor(rt[:, 5, :], rt[:, 2, :], pr[:, :, 2], ALU.min))
                link(vector.tensor_tensor(rt[:, 5, :], rt[:, 5, :], rt[:, 3, :], ALU.max))
                link(vector.tensor_tensor(rt[:, 6, :], rt[:, 4, :], rt[:, 5, :], ALU.add))
                link(vector.tensor_scalar(rt[:, 6, :], rt[:, 6, :], 1e-8, None, ALU.add))
                link(vector.reciprocal(rt[:, 6, :], rt[:, 6, :]))
                for choice in range(2):
                    link(vector.scalar_tensor_tensor(coef[:, :, choice, :], rt[:, 4 + choice, :].rearrange("p (b s) -> p b s", b=B),
                                                     1.0 / WS, rt[:, 6, :].rearrange("p (b s) -> p b s", b=B), ALU.mult, ALU.mult))

            def addition(k, step, codes_k, ws, before, done):
                a, factor = suma[:, k, :], WS if ws else 1.0
                if step > 1:
                    vec.wait_ge(done, before + step - 1)
                if step < ADDS:
                    other = term[:, 0, :] if step == 1 else a
                    ins = vector.scalar_tensor_tensor(a, term[:, step, :], NF4_CAPS[step - 1] * factor, other, ALU.min, ALU.add)
                else:
                    ins = vector.scalar_tensor_tensor(a, codes_k, NF4_SLOPE * factor, a, ALU.mult, ALU.subtract)
                ins.then_inc(done, 1)

            def attn_step(n, k, step):
                p = 4 * n + k
                if step <= ADDS:
                    vec.wait_ge(aterm, NTERM * p + min(step + 1, NTERM))
                    addition(k % 3, step, codes[:, k, :], 0, ADDS * p + ADDS, aread)
                    return
                blocks = "p (b c) -> p b c"
                target = (wa if k < 3 else w3)[:, col(n, 1), :].rearrange("p a d -> p (a d)")
                mine = suma[:, k % 3, :]
                if step == SCALE:
                    vec.wait_ge(aread, ADDS * p + 2 * ADDS)
                    dst = target if k in (0, 3) else mine
                    if k == 3:
                        vec.wait_ge(ascl_in, 32 * n + 32)
                        vector.scalar_tensor_tensor(dst, mine, NF4[0], scl[:, 0, :], ALU.add, ALU.mult).then_inc(ascaled, 1)
                    else:
                        scales = ascl[:, col(n, 1), k * NB:(k + 1) * NB].rearrange("p a b -> p (a b)")
                        vector.scalar_tensor_tensor(dst.rearrange(blocks, b=NB), mine.rearrange(blocks, b=NB), NF4[0],
                                                    scales.unsqueeze(2).to_broadcast([P, NB, D // NB]), ALU.add,
                                                    ALU.mult).then_inc(ascaled, 1)
                else:
                    vec.wait_ge(ascaled, p + 1)
                    vec.wait_ge(amerged, p + 4)
                    if k in (0, 3):
                        vec.wait_ge(aba_ps, 2 * n + (1 if k == 0 else 2))
                        other = ps[:, ABA + (k == 3), :]
                    else:
                        other = mine
                    vector.tensor_tensor(target, other, target, ALU.add).then_inc(amerged, 1)

            def w_low(n, w):
                vec.wait_ge(w_hi[w], n + 1)
                vector.scalar_tensor_tensor(wpair[:, w, 1, :, :].rearrange("p k f -> p (k f)"), wstage[:, w, :], WS,
                                            wpair[:, w, 0, :, :].rearrange("p k f -> p (k f)"), ALU.mult,
                                            ALU.subtract).then_inc(w_ready[w], 1)

            def stack_low(n):
                vec.wait_ge(stack_hi, 2)
                a, b_ = STACK_PARTS
                for p0, rows, (c0, width, scale) in ((64, 64, a), (32, 32, b_), (96, 32, b_)):
                    cols = col(c0 + n * (width // 4), width // 4)
                    vector.scalar_tensor_tensor(stack[p0:p0 + rows, cols], raw[p0:p0 + rows, cols], scale,
                                                stack[p0:p0 + rows, cols], ALU.mult, ALU.subtract).then_inc(stacks_ready, 1)

            for t in range(8):
                stats(t)
            aggregate(0)
            normalise(0)
            vec.wait_ge(eye_in, 16)
            vector.tensor_scalar(ident3[:, :], ident[:, :], 3.0, None, ALU.mult)
            vector.tensor_scalar(ident64[:, :], ident[:, :], WS, None, ALU.mult).then_inc(ident_ready, 1)
            vec.wait_ge(router_in, 16 * 4)
            vector.tensor_scalar(gw6[:, :, 0:E], gw[:, :, :], WS, None, ALU.mult).then_inc(gw_ready, 1)
            vec.wait_ge(gw_ready, 1)
            vector.scalar_tensor_tensor(gw6[:, :, E:2 * E], gw[:, :, :], WS, gw6[:, :, 0:E], ALU.mult,
                                        ALU.subtract).then_inc(gw_ready, 1)
            for t in range(8):
                token_low(t, t + 1)
                stats(t + 8)
            aggregate(1)
            abs_sums(0)
            router(0)
            normalise(1)
            token_low(8, 13)
            w_low(0, 0)
            token_low(13, 16)
            abs_sums(1)
            router(1)
            coefficients()
            vec.wait_ge(attn_in, 16 * 3)
            with vec.Fori(0, B) as b:
                for slot in range(2):
                    n = 2 * b + slot
                    for t in range(2 * KT):
                        c, f = t // KT, t % KT
                        vec.wait_ge(act_ready, 8 * n + t + 3)
                        vector.tensor_tensor(hmix[:, c, 1, f, :], act32[:, t % 2, :], hmix[:, c, 0, f, :],
                                             ALU.subtract).then_inc(hmix_ready, 1)
                        if t == 0:
                            w_low(n, 1)
                            vec.wait_ge(b2_in[slot], 32 * b + 32)
                            vector.tensor_scalar(b2p[0:33, slot, :], b2r[0:33, slot, :], WS, None, ALU.mult).then_inc(b2_hi, 1)
                            vec.wait_ge(b2_hi, n + 1)
                            vector.scalar_tensor_tensor(b2p[32:33, slot, :], b2r[32:33, slot, :], WS, b2p[32:33, slot, :],
                                                        ALU.mult, ALU.subtract).then_inc(b2_ready, 1)
                        if t == 3:
                            stack_low(n)
                        for k, step in VEC_ATTN[t]:
                            attn_step(n, k, step)
                    for s in range(8):
                        if s == 3:
                            w_low(n + 1, 0)
                        if slot == 1:
                            vec.wait_ge(out_ps, 8 * n + s + 1)
                            if s == 0:
                                vec.wait_ge(out0_read, 8 * b + 8)
                            vector.scalar_tensor_tensor(mix[:, s, :], ps[:, OUT + s % 2, :], coef[:, bass.ds(b, 1), 1, s],
                                                        mix[:, s, :], ALU.mult, ALU.add).then_inc(out1_read, 1)
                        for k, step in VEC_ATTN[8 + s]:
                            attn_step(n, k, step)

            def unit_step(u, slot, k, step):
                p = 3 * u + k
                if step <= ADDS:
                    vec.wait_ge(uterm, NTERM * p + min(step + 1, NTERM))
                    addition(k, step, codes[:, k, :], 1, ADDS * p + ADDS, uread)
                elif step == SCALE:
                    vec.wait_ge(uread, ADDS * p + 2 * ADDS)
                    vec.wait_ge(uscl_in[k], 32 * u + 32)
                    vector.scalar_tensor_tensor(suma[:, k, :], suma[:, k, :], NF4[0] * WS, scl[:, k, :], ALU.add,
                                                ALU.mult).then_inc(uscaled, 1)
                elif step == LORA:
                    vec.wait_ge(uscaled, p + 1)
                    vec.wait_ge(uba_ps, p + 1)
                    vector.tensor_tensor(suma[:, k, :], ps[:, UBA + k % 2, :], suma[:, k, :], ALU.add).then_inc(usum, 1)
                else:
                    vec.wait_ge(uhi, p + 1)
                    high = units[:, col(slot, 1), 0, k * PC:(k + 1) * PC].rearrange("p a n -> p (a n)")
                    low = units[:, col(slot, 1), 1, k * PC:(k + 1) * PC].rearrange("p a n -> p (a n)")
                    vector.tensor_tensor(low, suma[:, k, :], high, ALU.subtract).then_inc(uready, 1)

            for k in range(KT):
                for piece, step in VEC_UNIT0[k]:
                    unit_step(0, slot_of(0), piece, step)
                vec.wait_ge(c_hi, k + 1)
                vector.scalar_tensor_tensor(cpair[:, 1, k, :], ps[:, k, :], WS / 3.0, cpair[:, 0, k, :], ALU.mult,
                                            ALU.subtract).then_inc(c_ready, 1)
            for piece, step in VEC_UNIT0[KT]:
                unit_step(0, slot_of(0), piece, step)

            with vec.Fori(0, 2) as i:
                for t in range(8):
                    c, o = t // KT, t % KT
                    vec.wait_ge(x1_hi, 8 * i + t + 1)
                    cols = bass.ds(i * (2 * CH) + c * CH, CH)
                    vector.scalar_tensor_tensor(x1T[:, 1, o, cols], ps[:, t % 4, :], 1.0 / WS, x1T[:, 0, o, cols],
                                                ALU.mult, ALU.subtract).then_inc(x1_ready, 1)
                    for k, step in VEC_UNIT[8][t]:
                        unit_step(i + 1, i + slot_of(1), k, step)

            def hidden(q, r):
                vec.wait_ge(up_ps, q + 1)
                vec.wait_ge(silu_done, q + 1)
                vector.scalar_tensor_tensor(h32[:, r % 2, :], ps[:, UP, :], 1.0 / WS, sgate[:, r, :], ALU.mult,
                                            ALU.mult).then_inc(h_ready32, 1)

            def low(q, r):
                vec.wait_ge(h_hi, q + 1)
                vector.tensor_tensor(hffn[:, r, 1, :], h32[:, r % 2, :], hffn[:, r, 0, :], ALU.subtract).then_inc(h_ready, 1)

            def base(c, s, last):
                t = SPC * c + s
                gate, tokens = (last_g, last_x) if last else (fin_g, fin_x)
                mine = acc[:, col(t, 1), :].rearrange("p a d -> p (a d)")
                vec.wait_ge(fgate, t + 1)
                vector.scalar_tensor_tensor(mine, mine, 1.0 / WS, gate[:, s, :], ALU.mult, ALU.mult).then_inc(fscaled, 1)
                vec.wait_ge(fscaled, t + 1)
                if last:
                    vec.wait_ge(lx_in, 16)
                else:
                    vec.wait_ge(fx_in[s], 16 * c + 16)
                vector.tensor_tensor(tokens[:, s, :], mine, tokens[:, s, :], ALU.add).then_inc(fbase, 1)

            def output(c, it, s, last):
                t = SPC * c + s
                gate, tokens = (last_g, last_x) if last else (fin_g, fin_x)
                vec.wait_ge(down_read, SPC * it + s + 5)
                vec.wait_ge(fbase, t + 1)
                vector.tensor_tensor(tokens[:, s, :], gate[:, s, :], tokens[:, s, :], ALU.add).then_inc(fout, 1)

            def body(g, c, last):
                first, n = GROUPS[g]
                q = tiles_before[g] + c * n
                it = NCH * g + c
                new, width = GROUPS[g + 1] if g + 1 < len(GROUPS) else (None, 0)
                for v in range(1, n + 1):
                    steps = VEC_UNIT[n][v - 1] if new is not None and not (isinstance(c, int) and c >= width) else []
                    if not (last and v == n):
                        hidden(q + v, ring(v, n))
                    for k, step in steps[:2]:
                        unit_step(new + c, slot_of(new) + c, k, step)
                    if not (last and v == n):
                        low(q + v, ring(v, n))
                    for k, step in steps[2:]:
                        unit_step(new + c, slot_of(new) + c, k, step)
                    if new is None:
                        for s in FINAL_AT[last][v]:
                            base(c, s, last)
                if 0 < g < len(GROUPS) - 1:
                    for s in range(SPC):
                        vec.wait_ge(down_ps, SPC * it + s + 1)
                        mine = acc[:, col(SPC * c + s, 1), :].rearrange("p a d -> p (a d)")
                        vector.tensor_tensor(mine, ps[:, DOWN + s, :], mine, ALU.add).then_inc(down_read, 1)
                if new is None:
                    for s in range(SPC):
                        vec.wait_ge(down_ps, SPC * it + s + 1)
                        gate = (last_g if last else fin_g)[:, s, :]
                        vector.scalar_tensor_tensor(gate, ps[:, DOWN + s, :], 1.0 / WS, gate, ALU.mult,
                                                    ALU.mult).then_inc(down_read, 1)
                        if s:
                            output(c, it, s - 1, last)
                    output(c, it, SPC - 1, last)

            hidden(0, 0)
            low(0, 0)
            for g in range(len(GROUPS)):
                if g == 1:
                    vec.wait_ge(down_read, 4 + SPC * NCH)
                with vec.Fori(0, NCH - 1) as c:
                    body(g, c, False)
                body(g, NCH - 1, g == len(GROUPS) - 1)

        @block.tensor
        def _(pe):
            mm = nc.tensor.matmul

            def three(dst, stationary, moving, first, last):
                mm(dst, stationary(0), moving(0), start=first, stop=False)
                mm(dst, stationary(0), moving(1), start=False, stop=False)
                return mm(dst, stationary(1), moving(0), start=False, stop=last)

            pe.wait_ge(eye_in, 16)

            def transposes(b):
                for t in range(b * NST // B, (b + 1) * NST // B):
                    pe.wait_ge(xn_ready, t + 1)
                    if t >= TBANKS:
                        pe.wait_ge(xt_lo, t - TBANKS + 1)
                    for k in range(KT):
                        last = nc.tensor.transpose(ps[:, t % TBANKS, k * P:(k + 1) * P], xs[:, t, k * P:(k + 1) * P], ident[:, :])
                    last.then_inc(xt_ps, 1)

            def router(b):
                for t in range(b * NST // B, (b + 1) * NST // B):
                    pe.wait_ge(xt_lo, t + 1)
                    c0 = 2 * E * (t - b * NST // B)
                    for k in range(KT):
                        for h in range(2):
                            mm(ps[:, ROUTER + b, c0:c0 + 2 * E], xnT[:, h, k, t * P:(t + 1) * P], gw6[:, k, :],
                               start=(k == 0 and h == 0), stop=(k == KT - 1 and h == 1))
                pe.wait_ge(abs_ready, b + 1)
                mm(ps[:, ROUTER + b, STRENGTH:STRENGTH + 2], ones[:, :], abs_part[:, b, :], start=True,
                   stop=True).then_inc(router_ps, 1)

            transposes(0)
            pe.wait_ge(gw_ready, 2)
            router(0)
            transposes(1)
            router(1)
            pe.wait_ge(attn_in, 16 * 3)

            with pe.Fori(0, B) as b:
                for slot in range(2):
                    n = 2 * b + slot
                    pe.wait_ge(w_ready[0], n + 2)
                    for t in range(2 * KT):
                        c, f = t // KT, t % KT
                        pe.wait_ge(act_ready, 8 * n + t + 1)
                        for k in range(KT):
                            last = three(ps[:, PRE + t % 2, :], lambda h: wpair[:, 0, h, k, f * P:(f + 1) * P],
                                         lambda h: xnT[:, h, k, bass.ds(b * S + c * CH, CH)], k == 0, k == KT - 1)
                        last.then_inc(pre_ps, 1)
                        if t == 2:
                            pe.wait_ge(lb_in, 32 * n + 32)
                            pe.wait_ge(amerged, 4 * n + 4)
                            mm(ps[:, ABA, :], lb[0:3 * R, :], la[0:3 * R, :], start=True, stop=True).then_inc(aba_ps, 1)
                            mm(ps[:, ABA + 1, :], lb[64:64 + R, :], la[64:64 + R, :], start=True, stop=True).then_inc(aba_ps, 1)
                    pe.wait_ge(w_ready[1], n + 2)
                    pe.wait_ge(b2_ready, n + 1)
                    for s in range(8):
                        c = s // SPC
                        if slot == 0:
                            if s < 2:
                                pe.wait_ge(out1_read, 8 * b + 7 + s)
                            else:
                                pe.wait_ge(out0_read, 8 * b + s - 1)
                        elif s < 2:
                            pe.wait_ge(out0_read, 8 * b + 7 + s)
                        else:
                            pe.wait_ge(out1_read, 8 * b + 7 + s)
                        pe.wait_ge(hmix_ready, 8 * n + 4 * c + 6)
                        mm(ps[:, OUT + s % 2, :], ones16[0:33, :], b2p[0:33, slot, :], start=True, stop=False)
                        tok = slice((s % SPC) * P, (s % SPC + 1) * P)
                        for f in range(KT):
                            last = three(ps[:, OUT + s % 2, :], lambda h: hmix[:, c, h, f, tok],
                                         lambda h: wpair[:, 1, h, f, :], False, f == KT - 1)
                        last.then_inc(out_ps, 1)

            def unit_lora(u, pieces):
                for k in pieces:
                    pe.wait_ge(usum, 3 * u + (4 if k == 2 else 3))
                    if k < 2:
                        for i in range(KT):
                            last = mm(ps[:, UBA + k, i * P:(i + 1) * P], s_au[:, k, i * P:(i + 1) * P],
                                      s_bu[:, k, col(u * P, P)], start=True, stop=True)
                    else:
                        last = mm(ps[:, UBA, :], s_ad[:, col(u * P, P)], s_bd, start=True, stop=True)
                    last.then_inc(uba_ps, 1)

            pe.wait_ge(ident_ready, 1)
            pe.wait_ge(amerged, 4 * 4 + 4)
            pe.wait_ge(act_ready, 8 * 4 + 2)
            pe.wait_ge(stacks_ready, 3 * 4)
            unit_lora(0, (0, 1))
            for i in range(KT):
                if i == 2:
                    pe.wait_ge(out1_read, 8 * B + 8)
                    unit_lora(0, (2,))
                for k in range(KT):
                    mm(ps[:, i, :], wa[:, k, i * P:(i + 1) * P], w3[:, k, :], start=(k == 0), stop=False)
                mm(ps[:, i, i * P:(i + 1) * P], ident[:, :], ident3[:, :], start=False, stop=True).then_inc(c_ps, 1)

            pe.wait_ge(c_ready, KT)
            with pe.Fori(0, 2) as i:
                for t in range(8):
                    c, o = t // KT, t % KT
                    pe.wait_ge(x1_ready, 8 * i + t + 1)
                    for k in range(KT):
                        last = three(ps[:, t % 4, :], lambda h: cpair[:, h, k, o * P:(o + 1) * P],
                                     lambda h: xnT[:, h, k, bass.ds(i * (2 * CH) + c * CH, CH)], k == 0, k == KT - 1)
                    last.then_inc(x1_ps, 1)
                    if t == 0:
                        unit_lora(i + 1, (0, 1))
                    if t == 5:
                        unit_lora(i + 1, (2,))

            def gate_up(u, q, c):
                pe.wait_ge(uready, 3 * (u + 1))
                slot = slot_of(u)
                for g, (bank, done, read) in enumerate(((GATE, gate_ps, silu_done), (UP, up_ps, h_ready32))):
                    if not (isinstance(q, int) and q == 0):
                        pe.wait_ge(read, q)
                    for k in range(KT):
                        off = g * PC + k * P
                        last = three(ps[:, bank, :], lambda h: units[:, slot, h, off:off + P],
                                     lambda h: x1T[:, h, k, col(c * CH, CH)], k == 0, k == KT - 1)
                    last.then_inc(done, 1)

            def down(g, v, q, it, c):
                first, n = GROUPS[g]
                slot, r = slot_of(first + v), ring(v, n)
                pe.wait_ge(h_ready, q + 1)
                for s in range(SPC):
                    if v == 0:
                        pe.wait_ge(down_read, SPC * it + s + 1)
                    add_x1 = v == 0 and g == 0
                    if add_x1:
                        for k in range(KT):
                            for h in range(2):
                                mm(ps[:, DOWN + s, k * P:(k + 1) * P], x1T[:, h, k, col(c * CH + s * P, P)],
                                   ident64[:, :], start=(k == 0 and h == 0), stop=False)
                    last = three(ps[:, DOWN + s, :], lambda h: hffn[:, r, h, s * P:(s + 1) * P],
                                 lambda h: units[:, slot, h, 2 * PC:3 * PC], v == 0 and not add_x1, v == n - 1)
                    if v == n - 1:
                        last.then_inc(down_ps, 1)

            def body(g, c, peeled):
                first, n = GROUPS[g]
                q = tiles_before[g] + c * n
                it = NCH * g + c
                new, width = GROUPS[g + 1] if g + 1 < len(GROUPS) else (None, 0)
                for v in range(1, n + 1):
                    if v < n:
                        gate_up(first + v, q + v, c)
                    elif not peeled:
                        gate_up(first, q + n, c + 1)
                    elif new is not None:
                        gate_up(new, q + n, 0)
                    if new is not None and not (peeled and c >= width):
                        if v == 1:
                            unit_lora(new + c, (0, 1))
                        if v == (3 if n > 2 else 2):
                            unit_lora(new + c, (2,))
                    down(g, v - 1, q + v - 1, it, c)

            pe.wait_ge(x1_ready, 4 + 16)
            gate_up(0, 0, 0)
            for g in range(len(GROUPS)):
                with pe.Fori(0, NCH - 1) as c:
                    body(g, c, False)
                body(g, NCH - 1, True)


def kernel(**inputs):
    import numpy as np
    import concourse.bacc as bacc
    from concourse.bass_utils import run_bass_kernel_spmd

    a = {n: np.asarray(v) for n, v in inputs.items()}
    ca, sa = a["L0_attn_codes_attn"], a["L0_attn_scales_attn"]
    cg, sg = a["L0_attn_codes_gu"], a["L0_attn_scales_gu"]
    cd, sd = a["L0_attn_codes_down"], a["L0_attn_scales_down"]
    ah, ad = a["L0_attn_lora_A_h"], a["L0_attn_lora_A_down"]
    ba, bg, bd = a["L0_attn_lora_B_attn"], a["L0_attn_lora_B_gu"], a["L0_attn_lora_B_down"]

    codes4 = np.stack([ca[0], ca[1], ca[2], ca[3].T]).reshape(4, KT, P, D).transpose(1, 0, 2, 3)
    scales3 = sa[0:3].reshape(3, KT, P, NB).transpose(2, 1, 0, 3).reshape(P, KT, 3 * NB)
    scales_o = sa[3].T.reshape(KT, 2, D)
    cgt = cg.transpose(0, 2, 1).reshape(2, KT, P, UNITS, P).transpose(3, 0, 2, 1, 4).reshape(UNITS, 2, P, PC)
    cdt = cd.T.reshape(UNITS, 1, P, D)
    ucodes = np.concatenate([cgt, cdt], 1)
    sgt = sg.transpose(0, 2, 1).reshape(2, KT, 2, UNITS, P).transpose(3, 0, 2, 1, 4).reshape(UNITS, 2, 2, PC)
    sdt = sd.T.reshape(UNITS, 1, 2, D)
    uscales = np.concatenate([sgt, sdt], 1)
    pos = np.arange(T) % S
    share = np.stack([np.where(pos >= VISION, 1.0 / ((S - VISION) * D), 0.0),
                      np.where(pos < VISION, 1.0 / (VISION * D), 0.0)], -1).astype(np.float32)

    arrays = {
        "x": a["L0_attn_x"].reshape(T, D),
        "attn_codes": codes4, "attn_scales": scales3, "attn_scales_o": scales_o,
        "unit_codes": ucodes, "unit_scales": uscales,
        "lora_bt": ba[0:3].transpose(0, 2, 1).reshape(3 * R, KT, P).transpose(1, 0, 2),
        "lora_a": ah[0:3].reshape(3 * R, D),
        "lora_a3": ah[3].reshape(R, KT, P).transpose(1, 0, 2),
        "lora_bt3": ba[3].T,
        "lora_units": np.concatenate([ah[4:6].transpose(1, 0, 2).reshape(R, 2 * D), ad,
                                      bg.transpose(2, 0, 1).reshape(R, 2 * I), bd.T], 1),
        "gate_w": a["L0_ffn_gate_w"][0:D].reshape(KT, P, E).transpose(1, 0, 2),
        "gate_tail": a["L0_ffn_gate_w"][D:D + 1], "gate_b": a["L0_ffn_gate_b"].reshape(1, E),
        "w1": a["L0_ffn_w1"], "b1": a["L0_ffn_b1"].reshape(E, KT, P).transpose(0, 2, 1),
        "w2": a["L0_ffn_w2"], "b2": a["L0_ffn_b2"],
        "eye": np.eye(P, dtype=np.float32),
        "region": share.reshape(NST, P, 2).transpose(1, 0, 2),
    }
    arrays = {f"in_{n}": np.ascontiguousarray(v) for n, v in arrays.items()}
    nc = bacc.Bacc("TRN2", target_bir_lowering=False, num_devices=1)
    args = {n[3:]: nc.dram_tensor(n, v.shape, mybir.dt.from_np(v.dtype), kind="ExternalInput").ap()
            for n, v in arrays.items()}
    args["m_store"] = nc.dram_tensor("m_store", (B, NST // B, P, D), F32, kind="Internal").ap()
    args["out"] = nc.dram_tensor("out", (T, D), F32, kind="ExternalOutput").ap()
    build(nc, **args)
    r = run_bass_kernel_spmd(nc, [arrays], core_ids=[0])
    return r.results[0]["out"].reshape(B, S, D)
```
